# Optimizing a Trainium2 kernel written in Bass

```python
import numpy as np
import jax
import jax.numpy as jnp

def _softmax(x, axis=-1):
    return jax.nn.softmax(x, axis=axis)

def _gelu(x):
    return jax.nn.gelu(x, approximate=True)

def _silu(x):
    return jax.nn.silu(x)

def _sigmoid(x):
    return jax.nn.sigmoid(x)

def _layernorm(x, axis=-1, eps=1e-05):
    m = jnp.mean(x, axis=axis, keepdims=True)
    v = jnp.var(x, axis=axis, keepdims=True)
    return (x - m) / jnp.sqrt(v + eps)

def _scatter_add(tgt, idx, src, axis=0):
    return tgt.at[idx].add(src)

def _segment_sum(src, seg, n):
    return jax.ops.segment_sum(src, seg, n)
kernel_name = 'mk_vit_tower_d1_tok_img1024_r4_2f1231'

def setup_inputs(seed: int=0):
    np.random.seed(seed)
    _w = jnp.asarray

    def _rec_inputs():
        import jax
        import jax.numpy as jnp
        _rk = jax.random.key(seed)
        x = -0.00016672 + 0.999947 * jax.random.normal(jax.random.fold_in(_rk, 1), (16, 3, 96, 96), jnp.float32)
        return x
    x = _rec_inputs()

    def _L0_tok_setup():
        import jax, jax.numpy as jnp
        import numpy as np
        EMBED_DIM = 256
        IMAGE_SIZE = 96
        CHANNELS = 3
        PATCH = 16
        NUM_PATCHES = (IMAGE_SIZE // PATCH) ** 2
        PATCH_DIM = PATCH * PATCH * CHANNELS

        def _patchify(x, patch):
            B, C, H, W = x.shape
            hp, wp = (H // patch, W // patch)
            x = x.reshape(B, C, hp, patch, wp, patch)
            x = x.transpose(0, 2, 4, 1, 3, 5)
            return x.reshape(B, hp * wp, C * patch * patch)
        key = jax.random.key(seed)
        k_x, k_w, k_b, k_cls, k_pos = jax.random.split(key, 5)
        x = jax.random.normal(k_x, (64, CHANNELS, IMAGE_SIZE, IMAGE_SIZE), dtype=jnp.float32)
        W = jax.random.normal(k_w, (EMBED_DIM, PATCH_DIM), dtype=jnp.float32) / np.sqrt(PATCH_DIM)
        b = jax.random.normal(k_b, (EMBED_DIM,), dtype=jnp.float32) * 0.01
        cls_token = jax.random.normal(k_cls, (1, 1, EMBED_DIM), dtype=jnp.float32)
        pos_embedding = jax.random.normal(k_pos, (1, 1 + NUM_PATCHES, EMBED_DIM), dtype=jnp.float32)
        return {'x': x, 'W': W, 'b': b, 'cls_token': cls_token, 'pos_embedding': pos_embedding}
    _L0_tok_all = _L0_tok_setup()
    _L0_tok_in = {k: v for k, v in _L0_tok_all.items() if k in ('W', 'b', 'cls_token', 'pos_embedding')}
    del _L0_tok_all

    def _L0_attn_setup():
        import jax, jax.numpy as jnp
        import numpy as np
        B, T, HID = (16, 128, 256)
        NH, NKV, D = (8, 4, 128)
        THETA = 10000.0

        def _rotate_half(x):
            x1, x2 = (x[..., :x.shape[-1] // 2], x[..., x.shape[-1] // 2:])
            return jnp.concatenate((-x2, x1), axis=-1)
        key = jax.random.key(seed)
        k0, k1, k2, k3, k4 = jax.random.split(key, 5)
        s = 0.02
        return {'hidden_states': jax.random.normal(k0, (B, T, HID), dtype=jnp.float32), 'Wq': s * jax.random.normal(k1, (HID, NH * D), dtype=jnp.float32), 'Wk': s * jax.random.normal(k2, (HID, NKV * D), dtype=jnp.float32), 'Wv': s * jax.random.normal(k3, (HID, NKV * D), dtype=jnp.float32), 'Wo': s * jax.random.normal(k4, (NH * D, HID), dtype=jnp.float32)}
    _L0_attn_all = _L0_attn_setup()
    _L0_attn_in = {k: v for k, v in _L0_attn_all.items() if k in ('Wq', 'Wk', 'Wv', 'Wo')}
    del _L0_attn_all

    def _L0_ffn_setup():
        import jax, jax.numpy as jnp
        import numpy as np
        H_DIM, E_DIM = (256, 128)
        N_SHARED, N_ROUTED, TOP_K = (2, 16, 4)
        B, S = (4, 512)
        key = jax.random.key(seed)
        ks = jax.random.split(key, 6)
        sc = 1.0 / np.sqrt(H_DIM)
        ec = 1.0 / np.sqrt(E_DIM)
        return {'x': jax.random.normal(ks[0], (B, S, H_DIM), dtype=jnp.float32), 'shared_up': jax.random.uniform(ks[1], (N_SHARED, E_DIM, H_DIM), jnp.float32, -sc, sc), 'shared_down': jax.random.uniform(ks[2], (N_SHARED, H_DIM, E_DIM), jnp.float32, -ec, ec), 'routed_up': jax.random.uniform(ks[3], (N_ROUTED, E_DIM, H_DIM), jnp.float32, -sc, sc), 'routed_down': jax.random.uniform(ks[4], (N_ROUTED, H_DIM, E_DIM), jnp.float32, -ec, ec), 'router_w': jax.random.uniform(ks[5], (N_ROUTED, H_DIM), jnp.float32, -sc, sc)}
    _L0_ffn_all = _L0_ffn_setup()
    _L0_ffn_in = {k: v for k, v in _L0_ffn_all.items() if k in ('shared_up', 'shared_down', 'routed_up', 'routed_down', 'router_w')}
    del _L0_ffn_all
    return {'x': x, 'L0_tok_W': _L0_tok_in['W'], 'L0_tok_b': _L0_tok_in['b'], 'L0_tok_cls_token': _L0_tok_in['cls_token'], 'L0_tok_pos_embedding': _L0_tok_in['pos_embedding'], 'L0_attn_Wq': _L0_attn_in['Wq'], 'L0_attn_Wk': _L0_attn_in['Wk'], 'L0_attn_Wv': _L0_attn_in['Wv'], 'L0_attn_Wo': _L0_attn_in['Wo'], 'L0_ffn_shared_up': _L0_ffn_in['shared_up'], 'L0_ffn_shared_down': _L0_ffn_in['shared_down'], 'L0_ffn_routed_up': _L0_ffn_in['routed_up'], 'L0_ffn_routed_down': _L0_ffn_in['routed_down'], 'L0_ffn_router_w': _L0_ffn_in['router_w']}

def reference(x, L0_tok_W, L0_tok_b, L0_tok_cls_token, L0_tok_pos_embedding, L0_attn_Wq, L0_attn_Wk, L0_attn_Wv, L0_attn_Wo, L0_ffn_shared_up, L0_ffn_shared_down, L0_ffn_routed_up, L0_ffn_routed_down, L0_ffn_router_w):
    import jax
    import jax.numpy as jnp

    def _L0_tok_ref(x, W, b, cls_token, pos_embedding):
        import jax, jax.numpy as jnp
        import numpy as np
        EMBED_DIM = 256
        IMAGE_SIZE = 96
        CHANNELS = 3
        PATCH = 16
        NUM_PATCHES = (IMAGE_SIZE // PATCH) ** 2
        PATCH_DIM = PATCH * PATCH * CHANNELS

        def _patchify(x, patch):
            B, C, H, W = x.shape
            hp, wp = (H // patch, W // patch)
            x = x.reshape(B, C, hp, patch, wp, patch)
            x = x.transpose(0, 2, 4, 1, 3, 5)
            return x.reshape(B, hp * wp, C * patch * patch)
        B = x.shape[0]
        patches = _patchify(x, PATCH)
        tokens = jnp.einsum('bnd,ed->bne', patches, W) + b
        cls = jnp.broadcast_to(cls_token, (B, 1, EMBED_DIM))
        out = jnp.concatenate([cls, tokens], axis=1)
        return out + pos_embedding

    def _L0_attn_ref(hidden_states, Wq, Wk, Wv, Wo):
        import jax, jax.numpy as jnp
        import numpy as np
        B, T, HID = (16, 128, 256)
        NH, NKV, D = (8, 4, 128)
        THETA = 10000.0

        def _rotate_half(x):
            x1, x2 = (x[..., :x.shape[-1] // 2], x[..., x.shape[-1] // 2:])
            return jnp.concatenate((-x2, x1), axis=-1)
        b, t, _ = hidden_states.shape
        q = (hidden_states @ Wq).reshape(b, t, NH, D).transpose(0, 2, 1, 3)
        k = (hidden_states @ Wk).reshape(b, t, NKV, D).transpose(0, 2, 1, 3)
        v = (hidden_states @ Wv).reshape(b, t, NKV, D).transpose(0, 2, 1, 3)
        inv_freq = 1.0 / THETA ** (jnp.arange(0, D, 2, dtype=jnp.float32) / D)
        freqs = jnp.outer(jnp.arange(t, dtype=jnp.float32), inv_freq)
        emb = jnp.concatenate((freqs, freqs), axis=-1)
        cos, sin = (jnp.cos(emb), jnp.sin(emb))
        q = q * cos + _rotate_half(q) * sin
        k = k * cos + _rotate_half(k) * sin
        groups = NH // NKV
        k = jnp.repeat(k, groups, axis=1)
        v = jnp.repeat(v, groups, axis=1)
        scale = 1.0 / jnp.sqrt(jnp.float32(D))
        attn = jnp.einsum('bhtd,bhsd->bhts', q, k) * scale
        causal = jnp.triu(jnp.ones((t, t), dtype=bool), k=1)
        attn = jnp.where(causal, -jnp.inf, attn)
        attn = jax.nn.softmax(attn, axis=-1)
        out = jnp.einsum('bhts,bhsd->bhtd', attn, v)
        out = out.transpose(0, 2, 1, 3).reshape(b, t, NH * D)
        return out @ Wo

    def _L0_ffn_ref(x, shared_up, shared_down, routed_up, routed_down, router_w):
        import jax, jax.numpy as jnp
        import numpy as np
        H_DIM, E_DIM = (256, 128)
        N_SHARED, N_ROUTED, TOP_K = (2, 16, 4)
        B, S = (4, 512)
        b, s, h = x.shape
        xt = x.reshape(-1, h)
        up_s = jnp.einsum('th,seh->tse', xt, shared_up)
        shared = jnp.einsum('tse,she->th', jax.nn.gelu(up_s, approximate=False), shared_down)
        probs = jax.nn.softmax(xt @ router_w.T, axis=-1)
        topk_p, topk_i = jax.lax.top_k(probs, TOP_K)
        gate = jnp.zeros_like(probs).at[jnp.arange(xt.shape[0])[:, None], topk_i].add(topk_p)
        up_r = jnp.einsum('th,reh->tre', xt, routed_up)
        act = jax.nn.gelu(up_r, approximate=False) * gate[:, :, None]
        routed = jnp.einsum('tre,rhe->th', act, routed_down)
        return (shared + routed).reshape(b, s, h)
    h = _L0_tok_ref(x, L0_tok_W, L0_tok_b, L0_tok_cls_token, L0_tok_pos_embedding)
    h = h + _L0_attn_ref(_layernorm(h, axis=-1), L0_attn_Wq, L0_attn_Wk, L0_attn_Wv, L0_attn_Wo)
    h = h + _L0_ffn_ref(_layernorm(h, axis=-1), L0_ffn_shared_up, L0_ffn_shared_down, L0_ffn_routed_up, L0_ffn_routed_down, L0_ffn_router_w)
    return h

_drawn_inputs = setup_inputs


def setup_inputs(seed=0):
    import zlib

    import numpy as np

    out = dict(_drawn_inputs(seed))
    spreads = {}
    factors = {'L0_tok_b': 7.702, 'L0_attn_Wq': 8.0, 'L0_attn_Wk': 8.0}
    for name, (base, spread) in spreads.items():
        noise = np.random.default_rng([zlib.crc32(name.encode()), seed]).standard_normal(out[name].shape)
        drawn = base * np.exp(spread * noise) if base else spread * noise
        out[name] = jnp.asarray(drawn.astype(out[name].dtype))
    for name, factor in factors.items():
        out[name] = (out[name] * factor).astype(out[name].dtype)
    return out
```

```python
from contextlib import ExitStack

import concourse.bass as bass
from concourse import mybir

F32 = mybir.dt.float32
F32R = mybir.dt.float32r
BF16 = mybir.dt.bfloat16
ALU = mybir.AluOpType
ACT = mybir.ActivationFunctionType
AX_X = mybir.AxisListType.X

P = 128
IMAGES, PATCHES, TOKENS = 16, 36, 37
HALVES = 2
HT = IMAGES // HALVES * TOKENS
T = IMAGES * TOKENS
GROUPS = (3, 3, 2)
TILES = HALVES * len(GROUPS)
TN = [g * TOKENS for g in GROUPS] * HALVES
T0 = [sum(TN[:i]) for i in range(TILES)]
TMAX = max(TN)
HID = 256
KH = HID // P
KP = 3 * 16 * 16 // P
D = 128
NH, NKV = 8, 4
ROPED = NH + NKV
QUAD = 4
NSHARED, NROUTED, TOPK = 2, 16, 4
NEXP = NSHARED + NROUTED
EXPW = KH * P + HID
EARLY = NEXP // 2
SPLIT_RING = 4
ACT_RING = 3
SPLITS = 3
PADS = 4
MASKED = -1.0e30
EPS = 1e-5
QKV = (NH + 2 * NKV) * D
CHUNK = 512
SCALE = float(D) ** -0.5


def build(nc, xT, wpT, aux_w, aux_sel, w_qkv, w_o, w_ffn, w_r, cos_t, sin_t, ident_in, mask_in, sel_in, out):
    outer = ExitStack()
    with outer:
        def sb(name, shape, dt=F32, scope=outer):
            return scope.enter_context(nc.sbuf_tensor(name, shape, dt))

        def sem(name):
            return outer.enter_context(nc.semaphore(name))

        first = sb("first", [P, KP * T + KP * HID])
        x_sb = first[:, 0:KP * T].rearrange("p (b k t) -> p b k t", b=HALVES, k=KP)
        wp_sb = first[:, KP * T:].rearrange("p (k n) -> p k n", k=KP)
        heads_out = first[:, 0:NH * T].rearrange("p (h t) -> p h t", h=NH)
        auxw_sb = sb("auxw_sb", [TOKENS + 2, HID])
        auxs_sb = sb("auxs_sb", [TOKENS + 2, T])
        ident = sb("ident", [P, P])
        ident_b = sb("ident_b", [P, P], BF16)
        mask_f = sb("mask_f", [TMAX, TMAX])
        mask_b = sb("mask_b", [TMAX, QUAD, TMAX], BF16)
        sel_f = sb("sel_f", [SPLITS * NROUTED, NROUTED])
        sel_b = sb("sel_b", [SPLITS * NROUTED, NROUTED, P], BF16)
        cos_sb = sb("cos_sb", [P, HT])
        sin_sb = sb("sin_sb", [P, HT])
        wo_sb = sb("wo_sb", [P, NH, HID])
        wr_sb = sb("wr_sb", [P, KH, NROUTED])
        ffn_a = sb("ffn_a", [P, EARLY, EXPW])
        h = sb("h", [P, TILES, HID])
        hn = sb("hn", [P, 2, HID])
        hnT = sb("hnT", [P, KH, T])
        hnT_hi = sb("hnT_hi", [P, KH, T], F32R)
        hnT_lo = sb("hnT_lo", [P, KH, T], F32R)
        v_sb = sb("v_sb", [P, TILES, NKV * D])
        stats = sb("stats", [P, 2 * TILES, 6])
        mv = sb("mv", [P, 2 * TILES, 2])
        vare = sb("vare", [P, 2 * TILES])
        lnv = sb("lnv", [P, 2 * TILES])
        y0 = sb("y0", [P, 2 * TILES])
        y0y0 = sb("y0y0", [P, 2 * TILES])
        vyy = sb("vyy", [P, 2 * TILES])
        rstd = sb("rstd", [P, 2 * TILES])
        smax = sb("smax", [TMAX, TILES, NH])
        ssum = sb("ssum", [TMAX, TILES, NH])
        sinv = sb("sinv", [TMAX, TILES, NH])
        rmax = sb("rmax", [TMAX, TILES])
        rsum = sb("rsum", [TMAX, TILES])
        rinv = sb("rinv", [TMAX, TILES])
        rlog = sb("rlog", [TMAX, TILES, NROUTED])
        rexp = sb("rexp", [TMAX, TILES, NROUTED + PADS])
        rrest = sb("rrest", [TMAX, TILES, NROUTED + PADS])
        rtop = sb("rtop", [TMAX, TILES, 8])
        gate = sb("gate", [TMAX, 3, TILES, NROUTED])
        gparts = sb("gparts", [TMAX, TILES, SPLITS, NROUTED], BF16)
        gpartsT = sb("gpartsT", [SPLITS * NROUTED, T], BF16)

        att = ExitStack()
        wqkv_sb = sb("wqkv_sb", [P, KH, QKV], F32, att)
        wqkv_hi = sb("wqkv_hi", [P, KH, QKV], F32R, att)
        wqkv_lo = sb("wqkv_lo", [P, KH, QKV], F32R, att)
        qk = sb("qk", [P, ROPED, T], F32, att)
        swapped = sb("swapped", [P, 3, HT], F32, att)
        probs = sb("probs", [TMAX, 2, NH, TMAX], F32, att)
        probsT = sb("probsT", [TMAX, 2, NH, TMAX], F32, att)
        att.close()

        ffn = ExitStack()
        ffn_b = sb("ffn_b", [P, NEXP - EARLY, EXPW], F32, ffn)
        exp_hi = sb("exp_hi", [P, SPLIT_RING, EXPW], F32R, ffn)
        exp_lo = sb("exp_lo", [P, SPLIT_RING, EXPW], F32R, ffn)
        act = sb("act", [P, ACT_RING, HT], F32, ffn)
        act_hi = sb("act_hi", [P, ACT_RING, HT], F32R, ffn)
        act_lo = sb("act_lo", [P, ACT_RING, HT], F32R, ffn)
        yT = sb("yT", [P, KH, T], F32, ffn)
        ffn.close()

        bank = [outer.enter_context(nc.psum_tensor(f"bank{n}", [P, CHUNK], F32)) for n in range(8)]

        l_x = [[sem(f"l_x{b}{k}") for k in range(2)] for b in range(HALVES)]
        l_wp = [sem(f"l_wp{k}") for k in range(2)]
        l_aux = sem("l_aux")
        l_const = sem("l_const")
        l_qkv = [sem(f"l_qkv{c}") for c in range(QKV // CHUNK)]
        l_rope = sem("l_rope")
        l_wo = sem("l_wo")
        l_wr = sem("l_wr")
        l_ffn = [sem(f"l_ffn{n}") for n in range(6)]
        s_out = sem("s_out")
        c_identb = sem("c_identb")
        c_mask = sem("c_mask")
        c_sel = sem("c_sel")
        qkv_hi_made = sem("qkv_hi_made")
        qkv_lo_made = sem("qkv_lo_made")
        tok_made = sem("tok_made")
        h_kept = sem("h_kept")
        stats_made = sem("stats_made")
        mv_made = sem("mv_made")
        vare_made = sem("vare_made")
        ln_made = sem("ln_made")
        y0_made = sem("y0_made")
        yy_made = sem("yy_made")
        vyy_made = sem("vyy_made")
        rstd_made = sem("rstd_made")
        hn_made = sem("hn_made")
        hnT_turned = sem("hnT_turned")
        hnT_kept = sem("hnT_kept")
        hi_made = sem("hi_made")
        lo_made = sem("lo_made")
        qk_made = sem("qk_made")
        qk_swapped = sem("qk_swapped")
        qk_cos = sem("qk_cos")
        qk_sin = sem("qk_sin")
        qk_roped = sem("qk_roped")
        v_made = sem("v_made")
        v_kept = sem("v_kept")
        sc_made = sem("sc_made")
        sc_max = sem("sc_max")
        sc_less = sem("sc_less")
        sc_exp = sem("sc_exp")
        sc_sum = sem("sc_sum")
        sc_inv = sem("sc_inv")
        sc_norm = sem("sc_norm")
        pT_turned = sem("pT_turned")
        pT_kept = sem("pT_kept")
        pv_made = sem("pv_made")
        pv_kept = sem("pv_kept")
        wo_made = sem("wo_made")
        h_added = sem("h_added")
        rl_zeroed = sem("rl_zeroed")
        rl_made = sem("rl_made")
        r_max = sem("r_max")
        r_less = sem("r_less")
        r_pads = sem("r_pads")
        r_exp = sem("r_exp")
        r_sum = sem("r_sum")
        r_inv = sem("r_inv")
        r_top = sem("r_top")
        r_topped = sem("r_topped")
        r_rest = sem("r_rest")
        r_kept = sem("r_kept")
        r_gate = sem("r_gate")
        g_part = sem("g_part")
        g_turned = sem("g_turned")
        g_kept = sem("g_kept")
        exp_hi_made = sem("exp_hi_made")
        exp_lo_made = sem("exp_lo_made")
        up_made = sem("up_made")
        act_made = sem("act_made")
        gb_made = sem("gb_made")
        act_gated = sem("act_gated")
        act_hi_made = sem("act_hi_made")
        act_lo_made = sem("act_lo_made")
        y_made = sem("y_made")
        yT_kept = sem("yT_kept")
        y_turned = sem("y_turned")
        out_made = sem("out_made")

        def raw_expert(e):
            return ffn_a[:, e, :] if e < EARLY else ffn_b[:, e - EARLY, :]

        EXPERT_LOADS = [(0, 3), (3, 6), (6, 9), (9, 12), (12, 15), (15, 18)]

        ROPE_ORDER = [0, 8, 1, 2, 9, 3, 4, 10, 5, 6, 11, 7]

        def rope_unit(n):
            return n // ROPED, ROPE_ORDER[n % ROPED]

        def rope_bank(n):
            return 4 + n % 4 if n < ROPED else 4 + n % 2

        def rope_before(n):
            if n < ROPED:
                return n - 4 if n >= 4 else None
            return max(m for m in range(n) if rope_bank(m) == rope_bank(n))

        def rows(i):
            return slice(T0[i], T0[i] + TN[i])

        def half(b):
            return slice(b * HT, (b + 1) * HT)

        def quad(buf, i, c):
            return buf[0:TN[i], i % 2, QUAD * c:QUAD * c + QUAD, 0:TN[i]]

        def quad_bank(n, i):
            return bank[n][0:TN[i], 0:QUAD * TN[i]].rearrange("p (h t) -> p h t", h=QUAD)

        def per_head(buf, i, c):
            return buf[0:TN[i], i, QUAD * c:QUAD * c + QUAD].unsqueeze(2).broadcast_to([TN[i], QUAD, TN[i]])

        NU = NEXP * HALVES

        def gated_before(u):
            return max(0, u - NSHARED * HALVES)

        block = outer.enter_context(nc.Block())

        @block.sync
        def _(sp):
            for b in range(HALVES):
                for k in range(2):
                    ks = slice(k * KP // 2, (k + 1) * KP // 2)
                    if b == 0:
                        sp.dma_start(wp_sb[:, ks, :], wpT[:, ks, :]).then_inc(l_wp[k], 16)
                    sp.dma_start(x_sb[:, b, ks, :], xT[:, b, ks, :]).then_inc(l_x[b][k], 16)
            for c in (0, 2, 1, 3):
                cs = slice(c * CHUNK, (c + 1) * CHUNK)
                sp.dma_start(wqkv_sb[:, :, cs], w_qkv[:, c, :, :]).then_inc(l_qkv[c], 16)
            sp.dma_start(wo_sb[:], w_o).then_inc(l_wo, 16)
            for n, (a, z) in enumerate(EXPERT_LOADS):
                if a == EARLY:
                    sp.wait_ge(qk_made, HALVES * ROPED)
                    sp.wait_ge(v_made, TILES)
                dst = ffn_a[:, a:z, :] if a < EARLY else ffn_b[:, a - EARLY:z - EARLY, :]
                sp.dma_start(dst, w_ffn[:, a:z, :]).then_inc(l_ffn[n], 16)
            for i in range(TILES):
                sp.wait_ge(out_made, i + 1)
                sp.dma_start(out[rows(i), :], h[0:TN[i], i, :]).then_inc(s_out, 16)
            sp.wait_ge(s_out, 16 * TILES)

        @block.gpsimd
        def _(pool):
            for n, c in enumerate((0, 2, 1, 3)):
                cs = slice(c * CHUNK, (c + 1) * CHUNK)
                pool.wait_ge(l_qkv[c], 16)
                pool.wait_ge(qkv_hi_made, n + 1)
                nc.gpsimd.tensor_tensor(wqkv_lo[:, :, cs], wqkv_sb[:, :, cs], wqkv_hi[:, :, cs].bitcast(F32),
                                        ALU.subtract).then_inc(qkv_lo_made, 1)

            def sine(n):
                if n == 0:
                    pool.wait_ge(l_rope, 32)
                pool.wait_ge(qk_swapped, n + 1)
                nc.gpsimd.tensor_tensor(swapped[:, n % 3, :], swapped[:, n % 3, :], sin_sb[:],
                                        ALU.mult).then_inc(qk_sin, 1)

            def normalise(i):
                for c in range(2):
                    pool.wait_ge(sc_inv, 2 * i + c + 1)
                    pool.wait_ge(sc_exp, 2 * i + c + 1)
                    nc.gpsimd.tensor_tensor(quad(probs, i, c), quad(probs, i, c), per_head(sinv, i, c),
                                            ALU.mult).then_inc(sc_norm, 1)

            def low_parts(e):
                load = [n for n, (a, z) in enumerate(EXPERT_LOADS) if a <= e < z][0]
                pool.wait_ge(l_ffn[load], 16)
                pool.wait_ge(exp_hi_made, e + 1)
                nc.gpsimd.tensor_tensor(exp_lo[:, e % SPLIT_RING, :], raw_expert(e),
                                        exp_hi[:, e % SPLIT_RING, :].bitcast(F32),
                                        ALU.subtract).then_inc(exp_lo_made, 1)

            for n in range(ROPED):
                sine(n)
            for k in range(3):
                for n in range(ROPED + 4 * k, ROPED + 4 * k + 2):
                    sine(n)
                normalise(k)
                for n in range(ROPED + 4 * k + 2, ROPED + 4 * k + 4):
                    sine(n)
            for i in range(3, TILES):
                normalise(i)
            for e in range(NEXP):
                low_parts(e)

        @block.scalar
        def _(act_e):
            act_e.dma_start(auxw_sb[:], aux_w).then_inc(l_aux, 16)
            act_e.dma_start(auxs_sb[:], aux_sel).then_inc(l_aux, 16)
            act_e.dma_start(ident[:], ident_in).then_inc(l_const, 16)
            act_e.dma_start(mask_f[:], mask_in).then_inc(l_const, 16)
            act_e.dma_start(sel_f[:], sel_in).then_inc(l_const, 16)
            act_e.dma_start(cos_sb[:], cos_t).then_inc(l_rope, 16)
            act_e.dma_start(sin_sb[:], sin_t).then_inc(l_rope, 16)
            act_e.dma_start(wr_sb[:], w_r).then_inc(l_wr, 16)

            def keep_tokens(i):
                act_e.wait_ge(tok_made, i + 1)
                nc.scalar.activation(h[0:TN[i], i, :], bank[i % 2][0:TN[i], 0:HID], ACT.Copy).then_inc(h_kept, 1)

            def inv_std(n):
                r = slice(0, TN[n % TILES])
                act_e.wait_ge(vare_made, n + 1)
                nc.scalar.activation(lnv[r, n:n + 1], vare[r, n:n + 1], ACT.Ln).then_inc(ln_made, 1)
                act_e.wait_ge(ln_made, n + 1)
                nc.scalar.activation(y0[r, n:n + 1], lnv[r, n:n + 1], ACT.Exp, scale=-0.5).then_inc(y0_made, 1)

            def keep_turned(n):
                i = n % TILES
                act_e.wait_ge(hnT_turned, n + 1)
                if n >= TILES:
                    act_e.wait_ge(lo_made, i + 1)
                src = bank[(2 if n < TILES else 4) + i % 2][:, 0:KH * TN[i]].rearrange("p (k t) -> p k t", k=KH)
                nc.scalar.activation(hnT[:, :, rows(i)], src, ACT.Copy).then_inc(hnT_kept, 1)

            def swap(n):
                act_e.wait_ge(qk_made, n + 1)
                if n >= 3:
                    act_e.wait_ge(qk_roped, n - 2)
                ps = bank[rope_bank(n)]
                nc.scalar.activation(swapped[0:64, n % 3, :], ps[64:128, 0:HT], ACT.Copy)
                nc.scalar.activation(swapped[64:128, n % 3, :], ps[0:64, 0:HT], ACT.Copy).then_inc(qk_swapped, 1)

            def keep_v(i):
                act_e.wait_ge(v_made, i + 1)
                nc.scalar.activation(v_sb[0:TN[i], i, :], bank[i % 2][0:TN[i], :], ACT.Copy).then_inc(v_kept, 1)

            def exps(i, c):
                act_e.wait_ge(sc_less, 2 * i + c + 1)
                nc.scalar.activation(quad(probs, i, c), quad(probs, i, c), ACT.Exp, scale=SCALE).then_inc(sc_exp, 1)

            def keep_pT(i):
                for c in range(2):
                    act_e.wait_ge(pT_turned, 2 * i + c + 1)
                    if i >= 2:
                        act_e.wait_ge(pv_made, 2 * (i - 2) + c + 1)
                    nc.scalar.activation(quad(probsT, i, c), quad_bank(6 + c, i), ACT.Copy).then_inc(pT_kept, 1)

            def keep_pv(i):
                for c in range(2):
                    act_e.wait_ge(pv_made, 2 * i + c + 1)
                    src = bank[c][:, 0:QUAD * TN[i]].rearrange("p (h t) -> p h t", h=QUAD)
                    nc.scalar.activation(heads_out[:, QUAD * c:QUAD * c + QUAD, rows(i)], src,
                                         ACT.Copy).then_inc(pv_kept, 1)

            def gelu(u):
                e, b = divmod(u, HALVES)
                act_e.wait_ge(up_made, u + 1)
                if u >= ACT_RING:
                    act_e.wait_ge(act_lo_made, u - ACT_RING + 1)
                nc.scalar.activation(act[:, u % ACT_RING, :], bank[u % 2][:, 0:HT], ACT.Gelu).then_inc(act_made, 1)

            def act_high(u):
                r = u % ACT_RING
                if u < NSHARED * HALVES:
                    act_e.wait_ge(act_made, u + 1)
                else:
                    act_e.wait_ge(act_gated, gated_before(u) + 1)
                if u >= ACT_RING:
                    act_e.wait_ge(y_made, u - ACT_RING + 1)
                nc.scalar.activation(act_hi[:, r, :], act[:, r, :], ACT.Copy).then_inc(act_hi_made, 1)

            for i in range(TILES):
                keep_tokens(i)
                inv_std(i)
                if i:
                    keep_turned(i - 1)
            keep_turned(TILES - 1)
            for n in range(ROPED):
                swap(n)
            for i in range(TILES):
                keep_v(i)
            for k in range(3):
                if k:
                    keep_pT(k - 1)
                    exps(k, 0)
                    keep_pv(k - 1)
                    exps(k, 1)
                for n in range(4):
                    swap(ROPED + 4 * k + n)
                    if k == 0 and n < 2:
                        exps(k, n)
            exps(3, 0)
            exps(3, 1)
            keep_pT(2)
            keep_pv(2)
            inv_std(TILES)
            exps(4, 0)
            exps(4, 1)
            keep_pT(3)
            keep_pv(3)
            inv_std(TILES + 1)
            keep_turned(TILES)
            inv_std(TILES + 2)
            exps(5, 0)
            exps(5, 1)
            keep_pT(4)
            keep_pv(4)
            keep_turned(TILES + 1)
            inv_std(TILES + 3)
            keep_turned(TILES + 2)
            keep_pT(5)
            keep_pv(5)
            inv_std(TILES + 4)
            keep_turned(TILES + 3)
            inv_std(TILES + 5)
            keep_turned(TILES + 4)
            keep_turned(TILES + 5)
            act_e.wait_ge(r_less, 1)
            nc.scalar.activation(rexp[:, :, 0:NROUTED], rlog[:], ACT.Exp).then_inc(r_exp, 1)
            for u in range(NU):
                gelu(u)
                if u:
                    act_high(u - 1)
            act_high(NU - 1)
            for m in range(KH):
                act_e.wait_ge(y_made, NU - 1)
                nc.scalar.activation(yT[:, m, half(0)], bank[4 + m][:, 0:HT], ACT.Copy).then_inc(yT_kept, 1)
            act_e.wait_ge(y_made, NU)
            nc.scalar.activation(yT[:, 0, half(1)], bank[6][:, 0:HT], ACT.Copy).then_inc(yT_kept, 1)
            nc.scalar.activation(yT[:, 1, half(1)], bank[7][:, 0:HT], ACT.Copy).then_inc(yT_kept, 1)

        @block.vector
        def _(dve):
            def qkv_high(n, c):
                cs = slice(c * CHUNK, (c + 1) * CHUNK)
                dve.wait_ge(l_qkv[c], 16)
                nc.vector.tensor_copy(wqkv_hi[:, :, cs], wqkv_sb[:, :, cs]).then_inc(qkv_hi_made, 1)

            def norm_stats(n):
                i = n % TILES
                r = slice(0, TN[i])
                if n < TILES:
                    dve.wait_ge(h_kept, n + 1)
                else:
                    dve.wait_ge(h_added, i + 1)
                nc.vector.bn_stats(stats[r, n, :], h[r, i, :]).then_inc(stats_made, 1)
                dve.wait_ge(stats_made, n + 1)
                nc.vector.bn_aggr(mv[r, n, :], stats[r, n, :]).then_inc(mv_made, 1)
                dve.wait_ge(mv_made, n + 1)
                nc.vector.tensor_scalar(vare[r, n:n + 1], mv[r, n, 1:2], EPS, None, ALU.add).then_inc(vare_made, 1)

            def norm_apply(n):
                i = n % TILES
                r = slice(0, TN[i])
                dve.wait_ge(y0_made, n + 1)
                nc.vector.tensor_tensor(y0y0[r, n:n + 1], y0[r, n:n + 1], y0[r, n:n + 1],
                                        ALU.mult).then_inc(yy_made, 1)
                dve.wait_ge(yy_made, n + 1)
                nc.vector.tensor_scalar(vyy[r, n:n + 1], y0y0[r, n:n + 1], vare[r, n:n + 1], -0.5,
                                        ALU.mult, ALU.mult).then_inc(vyy_made, 1)
                dve.wait_ge(vyy_made, n + 1)
                nc.vector.scalar_tensor_tensor(out=rstd[r, n:n + 1], in0=vyy[r, n:n + 1], scalar=1.5,
                                               in1=y0[r, n:n + 1], op0=ALU.add, op1=ALU.mult).then_inc(rstd_made, 1)
                dve.wait_ge(rstd_made, n + 1)
                if n >= 2:
                    dve.wait_ge(hnT_turned, n - 1)
                nc.vector.tensor_scalar(hn[r, n % 2, :], h[r, i, :], mv[r, n, 0:1], rstd[r, n:n + 1],
                                        ALU.subtract, ALU.mult).then_inc(hn_made, 1)

            def split(n):
                i = n % TILES
                dve.wait_ge(hnT_kept, n + 1)
                if n >= TILES:
                    dve.wait_ge(qk_made, HALVES * ROPED)
                    dve.wait_ge(v_made, TILES)
                nc.vector.tensor_copy(hnT_hi[:, :, rows(i)], hnT[:, :, rows(i)]).then_inc(hi_made, 1)
                dve.wait_ge(hi_made, n + 1)
                nc.vector.tensor_tensor(hnT_lo[:, :, rows(i)], hnT[:, :, rows(i)],
                                        hnT_hi[:, :, rows(i)].bitcast(F32), ALU.subtract).then_inc(lo_made, 1)

            def cosine(n):
                b, head = rope_unit(n)
                if n == 0:
                    dve.wait_ge(l_rope, 32)
                dve.wait_ge(qk_swapped, n + 1)
                nc.vector.tensor_tensor(qk[:, head, half(b)], bank[rope_bank(n)][:, 0:HT], cos_sb[:],
                                        ALU.mult).then_inc(qk_cos, 1)

            def rope_add(n):
                b, head = rope_unit(n)
                dve.wait_ge(qk_cos, n + 1)
                dve.wait_ge(qk_sin, n + 1)
                nc.vector.tensor_tensor(qk[:, head, half(b)], qk[:, head, half(b)], swapped[:, n % 3, :],
                                        ALU.add).then_inc(qk_roped, 1)

            def less_max(i):
                for c in range(2):
                    dve.wait_ge(sc_made, 2 * i + c + 1)
                    nc.vector.tensor_reduce(smax[0:TN[i], i, QUAD * c:QUAD * c + QUAD], quad_bank(2 + c, i),
                                            AX_X, ALU.max).then_inc(sc_max, 1)
                for c in range(2):
                    dve.wait_ge(sc_max, 2 * i + c + 1)
                    if i >= 2:
                        dve.wait_ge(pT_turned, 2 * (i - 2) + c + 1)
                    nc.vector.tensor_tensor(quad(probs, i, c), quad_bank(2 + c, i), per_head(smax, i, c),
                                            ALU.subtract).then_inc(sc_less, 1)

            def inv_sum(i):
                for c in range(2):
                    dve.wait_ge(sc_exp, 2 * i + c + 1)
                    nc.vector.tensor_reduce(ssum[0:TN[i], i, QUAD * c:QUAD * c + QUAD], quad(probs, i, c),
                                            AX_X, ALU.add).then_inc(sc_sum, 1)
                for c in range(2):
                    dve.wait_ge(sc_sum, 2 * i + c + 1)
                    nc.vector.reciprocal(sinv[0:TN[i], i, QUAD * c:QUAD * c + QUAD],
                                         ssum[0:TN[i], i, QUAD * c:QUAD * c + QUAD]).then_inc(sc_inv, 1)

            def add_residual(i):
                dve.wait_ge(wo_made, i + 1)
                r = slice(0, TN[i])
                nc.vector.tensor_tensor(h[r, i, :], bank[4 + i % 2][r, 0:HID], h[r, i, :],
                                        ALU.add).then_inc(h_added, 1)

            def high_parts(e):
                load = [n for n, (a, z) in enumerate(EXPERT_LOADS) if a <= e < z][0]
                dve.wait_ge(l_ffn[load], 16)
                if e == 0:
                    dve.wait_ge(qk_made, HALVES * ROPED)
                    dve.wait_ge(v_made, TILES)
                if e >= SPLIT_RING:
                    dve.wait_ge(y_made, HALVES * (e - SPLIT_RING + 1))
                nc.vector.tensor_copy(exp_hi[:, e % SPLIT_RING, :], raw_expert(e)).then_inc(exp_hi_made, 1)

            def gates():
                logits = bank[2][0:TMAX, 0:TILES * NROUTED].rearrange("p (i r) -> p i r", i=TILES)
                spread = [TMAX, TILES, NROUTED]
                dve.wait_ge(rl_made, TILES)
                nc.vector.tensor_reduce(rmax[:], logits, AX_X, ALU.max).then_inc(r_max, 1)
                nc.vector.memset(rexp[:, :, NROUTED:], -1.0).then_inc(r_pads, 1)
                dve.wait_ge(r_max, 1)
                nc.vector.tensor_tensor(rlog[:], logits, rmax[:].unsqueeze(2).broadcast_to(spread),
                                        ALU.subtract).then_inc(r_less, 1)
                dve.wait_ge(r_exp, 1)
                dve.wait_ge(r_pads, 1)
                nc.vector.tensor_reduce(rsum[:], rexp[:, :, 0:NROUTED], AX_X, ALU.add).then_inc(r_sum, 1)
                for i in range(TILES):
                    nc.vector.max(rtop[:, i, :], rexp[:, i, :]).then_inc(r_top, 1)
                dve.wait_ge(r_sum, 1)
                nc.vector.reciprocal(rinv[:], rsum[:]).then_inc(r_inv, 1)
                dve.wait_ge(r_top, TILES)
                nc.vector.memset(rtop[:, :, TOPK:], -1.0).then_inc(r_topped, 1)
                dve.wait_ge(r_topped, 1)
                for i in range(TILES):
                    nc.vector.match_replace(rrest[:, i, :], rtop[:, i, :], rexp[:, i, :], 0.0).then_inc(r_rest, 1)
                dve.wait_ge(r_rest, TILES)
                nc.vector.tensor_tensor(rlog[:], rexp[:, :, 0:NROUTED], rrest[:, :, 0:NROUTED],
                                        ALU.subtract).then_inc(r_kept, 1)
                dve.wait_ge(r_kept, 1)
                dve.wait_ge(r_inv, 1)
                nc.vector.tensor_tensor(gate[:, 0], rlog[:], rinv[:].unsqueeze(2).broadcast_to(spread),
                                        ALU.mult).then_inc(r_gate, 1)
                dve.wait_ge(r_gate, 1)
                for s in range(SPLITS):
                    if s:
                        nc.vector.tensor_tensor(gate[:, s], gate[:, s - 1], gparts[:, :, s - 1, :],
                                                ALU.subtract).then_inc(g_part, 1)
                        dve.wait_ge(g_part, 2 * s)
                    nc.vector.tensor_copy(gparts[:, :, s, :], gate[:, s]).then_inc(g_part, 1)
                    dve.wait_ge(g_part, 2 * s + 1)

            def keep_gates():
                dve.wait_ge(g_turned, TILES)
                turned = bank[3][:].bitcast(BF16)
                for i in range(TILES):
                    nc.vector.tensor_copy(gpartsT[:, rows(i)],
                                          turned[0:SPLITS * NROUTED, i * P:i * P + TN[i]]).then_inc(g_kept, 1)

            def gated(u):
                dve.wait_ge(act_made, u + 1)
                dve.wait_ge(gb_made, gated_before(u) + 1)
                nc.vector.tensor_tensor(act[:, u % ACT_RING, :], act[:, u % ACT_RING, :],
                                        bank[2 + u % 2][:, 0:HT], ALU.mult).then_inc(act_gated, 1)

            def act_low(u):
                r = u % ACT_RING
                dve.wait_ge(act_hi_made, u + 1)
                nc.vector.tensor_tensor(act_lo[:, r, :], act[:, r, :], act_hi[:, r, :].bitcast(F32),
                                        ALU.subtract).then_inc(act_lo_made, 1)

            dve.wait_ge(l_const, 48)
            nc.vector.tensor_copy(ident_b[:], ident[:]).then_inc(c_identb, 1)
            nc.vector.tensor_copy(mask_b[:], mask_f[:].unsqueeze(1).broadcast_to([TMAX, QUAD, TMAX])).then_inc(c_mask, 1)
            nc.vector.tensor_copy(sel_b[:], sel_f[:].unsqueeze(2).broadcast_to([SPLITS * NROUTED, NROUTED, P])).then_inc(c_sel, 1)
            for i in range(TILES):
                norm_stats(i)
                if i:
                    split(i - 1)
                norm_apply(i)
                if i < 4:
                    qkv_high(i, (0, 2, 1, 3)[i])
            split(TILES - 1)
            for n in range(ROPED):
                cosine(n)
                if n:
                    rope_add(n - 1)
            rope_add(ROPED - 1)
            for k in range(3):
                less_max(k)
                cosine(ROPED + 4 * k)
                cosine(ROPED + 4 * k + 1)
                rope_add(ROPED + 4 * k)
                inv_sum(k)
                cosine(ROPED + 4 * k + 2)
                rope_add(ROPED + 4 * k + 1)
                cosine(ROPED + 4 * k + 3)
                rope_add(ROPED + 4 * k + 2)
                rope_add(ROPED + 4 * k + 3)
            less_max(3)
            inv_sum(3)
            add_residual(0)
            norm_stats(TILES)
            less_max(4)
            inv_sum(4)
            norm_apply(TILES)
            add_residual(1)
            norm_stats(TILES + 1)
            norm_apply(TILES + 1)
            split(TILES)
            add_residual(2)
            norm_stats(TILES + 2)
            less_max(5)
            inv_sum(5)
            norm_apply(TILES + 2)
            split(TILES + 1)
            add_residual(3)
            norm_stats(TILES + 3)
            split(TILES + 2)
            norm_apply(TILES + 3)
            add_residual(4)
            norm_stats(TILES + 4)
            split(TILES + 3)
            norm_apply(TILES + 4)
            dve.wait_ge(sc_less, 2 * TILES)
            nc.vector.memset(bank[2][0:TMAX, 0:TILES * NROUTED], 0.0).then_inc(rl_zeroed, 1)
            add_residual(5)
            norm_stats(TILES + 5)
            split(TILES + 4)
            norm_apply(TILES + 5)
            for e in range(2):
                high_parts(e)
            split(TILES + 5)
            gates()
            for u in range(NU):
                if u == NSHARED * HALVES:
                    keep_gates()
                if u >= NSHARED * HALVES:
                    gated(u)
                if u:
                    act_low(u - 1)
                if u % HALVES == 0 and u // HALVES + 2 < NEXP:
                    high_parts(u // HALVES + 2)
            act_low(NU - 1)
            for i in range(TILES):
                dve.wait_ge(y_turned, i + 1)
                r = slice(0, TN[i])
                nc.vector.tensor_tensor(h[r, i, :], bank[i % 4][r, 0:HID], h[r, i, :],
                                        ALU.add).then_inc(out_made, 1)

        @block.tensor
        def _(pe):
            def tokens(i):
                b, t = divmod(T0[i], HT)
                ps = bank[i % 2][0:TN[i], 0:HID]
                for k in range(KP):
                    if k % (KP // 2) == 0:
                        if i == 0:
                            pe.wait_ge(l_wp[2 * k // KP], 16)
                        if t == 0:
                            pe.wait_ge(l_x[b][2 * k // KP], 16)
                        if k == 0 and i >= 2:
                            pe.wait_ge(h_kept, i - 1)
                    nc.tensor.matmul(ps, x_sb[:, b, k, t:t + TN[i]], wp_sb[:, k, :], start=(k == 0), stop=False)
                if i == 0:
                    pe.wait_ge(l_aux, 32)
                nc.tensor.matmul(ps, auxs_sb[:, rows(i)], auxw_sb[:], start=False, stop=True).then_inc(tok_made, 1)

            def turn_norm(n):
                i = n % TILES
                if n == 0:
                    pe.wait_ge(l_const, 48)
                pe.wait_ge(hn_made, n + 1)
                if n < TILES:
                    if n >= 2:
                        pe.wait_ge(hnT_kept, n - 1)
                    ps = bank[2 + i % 2]
                else:
                    ps = bank[4 + i % 2]
                for k in range(KH):
                    last = nc.tensor.transpose(ps[:, k * TN[i]:(k + 1) * TN[i]],
                                               hn[0:TN[i], n % 2, k * P:(k + 1) * P], ident[0:TN[i], 0:TN[i]])
                last.then_inc(hnT_turned, 1)

            def three(ps, pairs):
                for n, (a_hi, a_lo, b_hi, b_lo) in enumerate(pairs):
                    for m, (a, b) in enumerate(((a_hi, b_hi), (a_hi, b_lo), (a_lo, b_hi))):
                        last = nc.tensor.matmul(ps, a, b, start=(n == 0 and m == 0),
                                                stop=(n == len(pairs) - 1 and m == 2))
                return last

            def project(n):
                b, head = rope_unit(n)
                if n == 0:
                    pe.wait_ge(lo_made, TILES // 2)
                if n == ROPED:
                    pe.wait_ge(lo_made, TILES)
                if n < ROPED:
                    pe.wait_ge(qkv_lo_made, (1, 3, 2)[head // 4])
                before = rope_before(n)
                if before is not None:
                    pe.wait_ge(qk_cos, before + 1)
                cs = slice(head * D, (head + 1) * D)
                three(bank[rope_bank(n)][:, 0:HT],
                      [(wqkv_hi[:, k, cs], wqkv_lo[:, k, cs], hnT_hi[:, k, half(b)], hnT_lo[:, k, half(b)])
                       for k in range(KH)]).then_inc(qk_made, 1)

            def values(i):
                pe.wait_ge(lo_made, TILES)
                pe.wait_ge(qkv_lo_made, 4)
                if i >= 2:
                    pe.wait_ge(v_kept, i - 1)
                else:
                    pe.wait_ge(h_kept, TILES)
                vs = slice(ROPED * D, QKV)
                three(bank[i % 2][0:TN[i], :],
                      [(hnT_hi[:, k, rows(i)], hnT_lo[:, k, rows(i)], wqkv_hi[:, k, vs], wqkv_lo[:, k, vs])
                       for k in range(KH)]).then_inc(v_made, 1)

            def scores(i):
                b = i // len(GROUPS)
                pe.wait_ge(qk_roped, ROPED * (b + 1))
                if i == 0:
                    pe.wait_ge(c_mask, 1)
                    pe.wait_ge(c_identb, 1)
                    pe.wait_ge(hnT_kept, TILES)
                for c in range(2):
                    if i:
                        pe.wait_ge(sc_less, 2 * (i - 1) + c + 1)
                    nc.tensor.matmul(quad_bank(2 + c, i), ident_b[0:TN[i], 0:TN[i]],
                                     mask_b[0:TN[i], :, 0:TN[i]], start=True, stop=False, skip_group_check=True)
                    for j in range(QUAD):
                        hd = QUAD * c + j
                        last = nc.tensor.matmul(bank[2 + c][0:TN[i], j * TN[i]:(j + 1) * TN[i]],
                                                qk[:, hd, rows(i)], qk[:, NH + hd * NKV // NH, rows(i)],
                                                start=False, stop=(j == QUAD - 1), skip_group_check=True)
                    last.then_inc(sc_made, 1)

            def turn_probs(i):
                for c in range(2):
                    pe.wait_ge(sc_norm, 2 * i + c + 1)
                    if i:
                        pe.wait_ge(pT_kept, 2 * (i - 1) + c + 1)
                    else:
                        pe.wait_ge(qk_cos, ROPED)
                    for j in range(QUAD):
                        last = nc.tensor.transpose(bank[6 + c][0:TN[i], j * TN[i]:(j + 1) * TN[i]],
                                                   probs[0:TN[i], i % 2, QUAD * c + j, 0:TN[i]],
                                                   ident[0:TN[i], 0:TN[i]])
                    last.then_inc(pT_turned, 1)

            def attend(i):
                for c in range(2):
                    pe.wait_ge(pT_kept, 2 * i + c + 1)
                    if i:
                        pe.wait_ge(pv_kept, 2 * (i - 1) + c + 1)
                    else:
                        pe.wait_ge(v_kept, TILES)
                    for j in range(2):
                        kv = 2 * c + j
                        last = nc.tensor.matmul(
                            bank[c][:, 2 * j * TN[i]:2 * (j + 1) * TN[i]].rearrange("p (h t) -> p h t", h=2),
                            v_sb[0:TN[i], i, kv * D:(kv + 1) * D],
                            probsT[0:TN[i], i % 2, 2 * kv:2 * kv + 2, 0:TN[i]], start=True, stop=True)
                    last.then_inc(pv_made, 1)

            def project_out(i):
                pe.wait_ge(pv_kept, 2 * (i + 1))
                if i == 0:
                    pe.wait_ge(l_wo, 16)
                    pe.wait_ge(qk_cos, HALVES * ROPED)
                if i >= 2:
                    pe.wait_ge(hnT_kept, TILES + i - 1)
                for k in range(NH):
                    last = nc.tensor.matmul(bank[4 + i % 2][0:TN[i], 0:HID], heads_out[:, k, rows(i)], wo_sb[:, k, :],
                                            start=(k == 0), stop=(k == NH - 1))
                last.then_inc(wo_made, 1)

            def route(i):
                if i == 0:
                    pe.wait_ge(l_wr, 16)
                    pe.wait_ge(rl_zeroed, 1)
                pe.wait_ge(hnT_kept, TILES + i + 1)
                for k in range(KH):
                    last = nc.tensor.matmul(bank[2][0:TN[i], i * NROUTED:(i + 1) * NROUTED], hnT[:, k, rows(i)],
                                            wr_sb[:, k, :], start=(k == 0), stop=(k == KH - 1))
                last.then_inc(rl_made, 1)

            def turn_gates():
                pe.wait_ge(g_part, 2 * SPLITS - 1)
                turned = bank[3][:].bitcast(BF16)
                for i in range(TILES):
                    nc.tensor.transpose(turned[0:SPLITS * NROUTED, i * P:i * P + TN[i]],
                                        gparts[0:TN[i], i].rearrange("p s r -> p (s r)"),
                                        ident_b[0:TN[i], 0:TN[i]]).then_inc(g_turned, 1)

            def up(u):
                e, b = divmod(u, HALVES)
                s = e % SPLIT_RING
                if b == 0:
                    pe.wait_ge(exp_lo_made, e + 1)
                pe.wait_ge(lo_made, TILES + (b + 1) * TILES // 2)
                if u >= 2:
                    pe.wait_ge(act_made, u - 1)
                else:
                    pe.wait_ge(pv_kept, 2 * TILES)
                three(bank[u % 2][:, 0:HT],
                      [(exp_hi[:, s, k * P:(k + 1) * P], exp_lo[:, s, k * P:(k + 1) * P],
                        hnT_hi[:, k, half(b)], hnT_lo[:, k, half(b)]) for k in range(KH)]).then_inc(up_made, 1)
                if e >= NSHARED:
                    if u == NSHARED * HALVES:
                        pe.wait_ge(g_kept, TILES)
                        pe.wait_ge(c_sel, 1)
                    if gated_before(u) >= 2:
                        pe.wait_ge(act_gated, gated_before(u) - 1)
                    nc.tensor.matmul(bank[2 + u % 2][:, 0:HT], sel_b[:, e - NSHARED, :], gpartsT[:, half(b)],
                                     start=True, stop=True).then_inc(gb_made, 1)

            def down(u):
                e, b = divmod(u, HALVES)
                s, r = e % SPLIT_RING, u % ACT_RING
                if u == 0:
                    pe.wait_ge(hnT_kept, 2 * TILES)
                pe.wait_ge(act_lo_made, u + 1)
                for m in range(KH):
                    ws = slice(KH * P + m * P, KH * P + (m + 1) * P)
                    for n, (w, a) in enumerate(((exp_hi, act_hi), (exp_hi, act_lo), (exp_lo, act_hi))):
                        last = nc.tensor.matmul(bank[4 + 2 * b + m][:, 0:HT], w[:, s, ws], a[:, r, :],
                                                start=(e == 0 and n == 0), stop=(e == NEXP - 1 and n == 2))
                last.then_inc(y_made, 1)

            def turn_back(i):
                b = i // len(GROUPS)
                pe.wait_ge(yT_kept, KH * (b + 1))
                if i < 4:
                    pe.wait_ge(act_made, NU)
                    pe.wait_ge(act_gated, NROUTED * HALVES)
                else:
                    pe.wait_ge(out_made, i - 3)
                for m in range(KH):
                    last = nc.tensor.transpose(bank[i % 4][0:TN[i], m * P:(m + 1) * P], yT[:, m, rows(i)], ident[:])
                last.then_inc(y_turned, 1)

            for i in range(TILES):
                tokens(i)
                if i:
                    turn_norm(i - 1)
            turn_norm(TILES - 1)
            for n in range(ROPED):
                project(n)
            for i in range(TILES):
                values(i)
            for k in range(3):
                scores(k)
                if k:
                    turn_probs(k - 1)
                    attend(k - 1)
                for n in range(ROPED + 4 * k, ROPED + 4 * k + 4):
                    project(n)
            scores(3)
            turn_probs(2)
            attend(2)
            project_out(0)
            project_out(1)
            scores(4)
            turn_norm(TILES)
            turn_probs(3)
            attend(3)
            project_out(2)
            turn_norm(TILES + 1)
            scores(5)
            turn_probs(4)
            attend(4)
            project_out(3)
            turn_norm(TILES + 2)
            turn_probs(5)
            attend(5)
            project_out(4)
            turn_norm(TILES + 3)
            project_out(5)
            turn_norm(TILES + 4)
            turn_norm(TILES + 5)
            for i in range(TILES):
                route(i)
            LAG = 2
            for u in range(NU + LAG):
                if u < NU:
                    if u == NSHARED * HALVES:
                        turn_gates()
                    up(u)
                if u >= LAG:
                    down(u - LAG)
            for i in range(TILES):
                turn_back(i)


def kernel(x, L0_tok_W, L0_tok_b, L0_tok_cls_token, L0_tok_pos_embedding, L0_attn_Wq, L0_attn_Wk, L0_attn_Wv,
           L0_attn_Wo, L0_ffn_shared_up, L0_ffn_shared_down, L0_ffn_routed_up, L0_ffn_routed_down,
           L0_ffn_router_w):
    import numpy as np
    import concourse.bacc as bacc
    from concourse.bass_utils import run_bass_kernel_spmd

    side = 96 // 16
    px = np.asarray(x).reshape(IMAGES, 3, side, 16, side, 16).transpose(1, 3, 5, 0, 2, 4)
    px = px.reshape(KP, P, IMAGES, PATCHES)
    xT = np.zeros((KP, P, IMAGES, TOKENS), px.dtype)
    xT[:, :, :, 1:] = px
    xT = xT.reshape(KP, P, HALVES, HT).transpose(1, 2, 0, 3)
    wpT = np.asarray(L0_tok_W).reshape(HID, KP, P).transpose(2, 1, 0)

    aux_w = np.concatenate([np.asarray(L0_tok_pos_embedding)[0], np.asarray(L0_tok_b)[None],
                            np.asarray(L0_tok_cls_token)[0]])
    one = np.zeros((TOKENS + 2, TOKENS), np.float32)
    one[:TOKENS] = np.eye(TOKENS)
    one[TOKENS, 1:] = 1
    one[TOKENS + 1, 0] = 1
    aux_sel = np.tile(one, (1, IMAGES))

    w_qkv = np.concatenate([np.asarray(L0_attn_Wq), np.asarray(L0_attn_Wk), np.asarray(L0_attn_Wv)], axis=1)
    w_qkv = w_qkv.reshape(KH, P, QKV // CHUNK, CHUNK).transpose(1, 2, 0, 3)
    w_o = np.asarray(L0_attn_Wo).reshape(NH, P, HID).transpose(1, 0, 2)
    ups = np.concatenate([np.asarray(L0_ffn_shared_up), np.asarray(L0_ffn_routed_up)])
    downs = np.concatenate([np.asarray(L0_ffn_shared_down), np.asarray(L0_ffn_routed_down)])
    ups = ups.reshape(NEXP, P, KH, P).transpose(3, 0, 2, 1).reshape(P, NEXP, KH * P)
    w_ffn = np.concatenate([ups, downs.transpose(2, 0, 1)], axis=2)
    w_r = np.asarray(L0_ffn_router_w).reshape(NROUTED, KH, P).transpose(2, 1, 0)

    inv_freq = (1.0 / 10000.0 ** (np.arange(0, D, 2, dtype=np.float32) / np.float32(D))).astype(np.float32)
    freqs = np.outer(np.arange(TOKENS, dtype=np.float32), inv_freq)
    emb = np.concatenate([freqs, freqs], axis=1).T
    sign = np.where(np.arange(D) < D // 2, -1.0, 1.0)[:, None]
    cos_t = np.tile(np.cos(emb), (1, IMAGES // HALVES))
    sin_t = np.tile(np.sin(emb) * sign, (1, IMAGES // HALVES))
    image, place = np.divmod(np.arange(TMAX), TOKENS)
    allowed = (image[:, None] == image[None]) & (place[None] <= place[:, None])
    mask = np.where(allowed, 0.0, MASKED)
    sel = np.tile(np.eye(NROUTED), (SPLITS, 1))

    arrays = {
        "xT": xT, "wpT": wpT, "aux_w": aux_w, "aux_sel": aux_sel, "w_qkv": w_qkv, "w_o": w_o, "w_ffn": w_ffn,
        "w_r": w_r, "cos_t": cos_t.astype(np.float32), "sin_t": sin_t.astype(np.float32),
        "ident_in": np.eye(P, dtype=np.float32), "mask_in": mask.astype(np.float32), "sel_in": sel.astype(np.float32),
    }
    arrays = {name: np.ascontiguousarray(a) for name, a in arrays.items()}
    nc = bacc.Bacc("TRN2", target_bir_lowering=False, num_devices=1)
    args = [nc.dram_tensor(name, a.shape, mybir.dt.from_np(a.dtype), kind="ExternalInput").ap()
            for name, a in arrays.items()]
    out = nc.dram_tensor("out", (T, HID), F32, kind="ExternalOutput").ap()
    build(nc, *args, out)
    got = run_bass_kernel_spmd(nc, [arrays], core_ids=[0]).results[0]["out"]
    return got.reshape(IMAGES, TOKENS, HID)
```

```python
from contextlib import ExitStack

import concourse.bass as bass
from concourse import mybir

F32 = mybir.dt.float32
F32R = mybir.dt.float32r
BF16 = mybir.dt.bfloat16
ALU = mybir.AluOpType
ACT = mybir.ActivationFunctionType
AX_X = mybir.AxisListType.X

P = 128
IMAGES, PATCHES, TOKENS = 16, 36, 37
HALVES = 2
HT = IMAGES // HALVES * TOKENS
T = IMAGES * TOKENS
GROUPS = (3, 3, 2)
TILES = HALVES * len(GROUPS)
TN = [g * TOKENS for g in GROUPS] * HALVES
T0 = [sum(TN[:i]) for i in range(TILES)]
TMAX = max(TN)
HID = 256
KH = HID // P
KP = 3 * 16 * 16 // P
D = 128
NH, NKV = 8, 4
ROPED = NH + NKV
QUAD = 4
NSHARED, NROUTED, TOPK = 2, 16, 4
NEXP = NSHARED + NROUTED
EXPW = KH * P + HID
EARLY = NEXP // 2
SPLIT_RING = 4
ACT_RING = 3
SPLITS = 3
PADS = 4
MASKED = -1.0e30
EPS = 1e-5
QKV = (NH + 2 * NKV) * D
CHUNK = 512
SCALE = float(D) ** -0.5


def build(nc, xT, wpT, aux_w, aux_sel, w_qkv, w_o, w_ffn, w_r, cos_t, sin_t, ident_in, mask_in, sel_in, out):
    outer = ExitStack()
    with outer:
        def sb(name, shape, dt=F32, scope=outer):
            return scope.enter_context(nc.sbuf_tensor(name, shape, dt))

        def sem(name):
            return outer.enter_context(nc.semaphore(name))

        first = sb("first", [P, KP * T + KP * HID])
        x_sb = first[:, 0:KP * T].rearrange("p (b k t) -> p b k t", b=HALVES, k=KP)
        wp_sb = first[:, KP * T:].rearrange("p (k n) -> p k n", k=KP)
        heads_out = first[:, 0:NH * T].rearrange("p (h t) -> p h t", h=NH)
        auxw_sb = sb("auxw_sb", [TOKENS + 2, HID])
        auxs_sb = sb("auxs_sb", [TOKENS + 2, T])
        ident = sb("ident", [P, P])
        ident_b = sb("ident_b", [P, P], BF16)
        mask_f = sb("mask_f", [TMAX, TMAX])
        mask_b = sb("mask_b", [TMAX, QUAD, TMAX], BF16)
        sel_f = sb("sel_f", [SPLITS * NROUTED, NROUTED])
        sel_b = sb("sel_b", [SPLITS * NROUTED, NROUTED, P], BF16)
        cos_sb = sb("cos_sb", [P, HT])
        sin_sb = sb("sin_sb", [P, HT])
        wo_sb = sb("wo_sb", [P, NH, HID])
        wr_sb = sb("wr_sb", [P, KH, NROUTED])
        ffn_a = sb("ffn_a", [P, EARLY, EXPW])
        h = sb("h", [P, TILES, HID])
        hn = sb("hn", [P, 2, HID])
        hnT = sb("hnT", [P, KH, T])
        hnT_hi = sb("hnT_hi", [P, KH, T], F32R)
        hnT_lo = sb("hnT_lo", [P, KH, T], F32R)
        v_sb = sb("v_sb", [P, TILES, NKV * D])
        stats = sb("stats", [P, 2 * TILES, 6])
        mv = sb("mv", [P, 2 * TILES, 2])
        vare = sb("vare", [P, 2 * TILES])
        lnv = sb("lnv", [P, 2 * TILES])
        y0 = sb("y0", [P, 2 * TILES])
        y0y0 = sb("y0y0", [P, 2 * TILES])
        vyy = sb("vyy", [P, 2 * TILES])
        rstd = sb("rstd", [P, 2 * TILES])
        smax = sb("smax", [TMAX, TILES, NH])
        ssum = sb("ssum", [TMAX, TILES, NH])
        sinv = sb("sinv", [TMAX, TILES, NH])
        rmax = sb("rmax", [TMAX, TILES])
        rsum = sb("rsum", [TMAX, TILES])
        rinv = sb("rinv", [TMAX, TILES])
        rlog = sb("rlog", [TMAX, TILES, NROUTED])
        rexp = sb("rexp", [TMAX, TILES, NROUTED + PADS])
        rrest = sb("rrest", [TMAX, TILES, NROUTED + PADS])
        rtop = sb("rtop", [TMAX, TILES, 8])
        gate = sb("gate", [TMAX, 3, TILES, NROUTED])
        gparts = sb("gparts", [TMAX, TILES, SPLITS, NROUTED], BF16)
        gpartsT = sb("gpartsT", [SPLITS * NROUTED, T], BF16)

        att = ExitStack()
        wqkv_sb = sb("wqkv_sb", [P, KH, QKV], F32, att)
        wqkv_hi = sb("wqkv_hi", [P, KH, QKV], F32R, att)
        wqkv_lo = sb("wqkv_lo", [P, KH, QKV], F32R, att)
        qk = sb("qk", [P, ROPED, T], F32, att)
        swapped = sb("swapped", [P, 3, HT], F32, att)
        probs = sb("probs", [TMAX, 2, NH, TMAX], F32, att)
        probsT = sb("probsT", [TMAX, 2, NH, TMAX], F32, att)
        att.close()

        ffn = ExitStack()
        ffn_b = sb("ffn_b", [P, NEXP - EARLY, EXPW], F32, ffn)
        exp_hi = sb("exp_hi", [P, SPLIT_RING, EXPW], F32R, ffn)
        exp_lo = sb("exp_lo", [P, SPLIT_RING, EXPW], F32R, ffn)
        act = sb("act", [P, ACT_RING, HT], F32, ffn)
        act_hi = sb("act_hi", [P, ACT_RING, HT], F32R, ffn)
        act_lo = sb("act_lo", [P, ACT_RING, HT], F32R, ffn)
        yT = sb("yT", [P, KH, T], F32, ffn)
        ffn.close()

        bank = [outer.enter_context(nc.psum_tensor(f"bank{n}", [P, CHUNK], F32)) for n in range(8)]

        l_x = [[sem(f"l_x{b}{k}") for k in range(2)] for b in range(HALVES)]
        l_wp = [sem(f"l_wp{k}") for k in range(2)]
        l_aux = sem("l_aux")
        l_const = sem("l_const")
        l_qkv = [sem(f"l_qkv{c}") for c in range(QKV // CHUNK)]
        l_rope = sem("l_rope")
        l_wo = sem("l_wo")
        l_wr = sem("l_wr")
        l_ffn = [sem(f"l_ffn{n}") for n in range(6)]
        s_out = sem("s_out")
        c_identb = sem("c_identb")
        c_mask = sem("c_mask")
        c_sel = sem("c_sel")
        qkv_hi_made = sem("qkv_hi_made")
        qkv_lo_made = sem("qkv_lo_made")
        tok_made = sem("tok_made")
        h_kept = sem("h_kept")
        stats_made = sem("stats_made")
        mv_made = sem("mv_made")
        vare_made = sem("vare_made")
        ln_made = sem("ln_made")
        y0_made = sem("y0_made")
        yy_made = sem("yy_made")
        vyy_made = sem("vyy_made")
        rstd_made = sem("rstd_made")
        hn_made = sem("hn_made")
        hnT_turned = sem("hnT_turned")
        hnT_kept = sem("hnT_kept")
        hi_made = sem("hi_made")
        lo_made = sem("lo_made")
        qk_made = sem("qk_made")
        qk_swapped = sem("qk_swapped")
        qk_cos = sem("qk_cos")
        qk_sin = sem("qk_sin")
        qk_roped = sem("qk_roped")
        v_made = sem("v_made")
        v_kept = sem("v_kept")
        sc_made = sem("sc_made")
        sc_max = sem("sc_max")
        sc_less = sem("sc_less")
        sc_exp = sem("sc_exp")
        sc_sum = sem("sc_sum")
        sc_inv = sem("sc_inv")
        sc_norm = sem("sc_norm")
        pT_turned = sem("pT_turned")
        pT_kept = sem("pT_kept")
        pv_made = sem("pv_made")
        pv_kept = sem("pv_kept")
        wo_made = sem("wo_made")
        h_added = sem("h_added")
        rl_zeroed = sem("rl_zeroed")
        rl_made = sem("rl_made")
        r_max = sem("r_max")
        r_less = sem("r_less")
        r_pads = sem("r_pads")
        r_exp = sem("r_exp")
        r_sum = sem("r_sum")
        r_inv = sem("r_inv")
        r_top = sem("r_top")
        r_topped = sem("r_topped")
        r_rest = sem("r_rest")
        r_kept = sem("r_kept")
        r_gate = sem("r_gate")
        g_part = sem("g_part")
        g_turned = sem("g_turned")
        g_kept = sem("g_kept")
        exp_hi_made = sem("exp_hi_made")
        exp_lo_made = sem("exp_lo_made")
        up_made = sem("up_made")
        act_made = sem("act_made")
        gb_made = sem("gb_made")
        act_gated = sem("act_gated")
        act_hi_made = sem("act_hi_made")
        act_lo_made = sem("act_lo_made")
        y_made = sem("y_made")
        yT_kept = sem("yT_kept")
        y_turned = sem("y_turned")
        out_made = sem("out_made")

        def raw_expert(e):
            return ffn_a[:, e, :] if e < EARLY else ffn_b[:, e - EARLY, :]

        EXPERT_LOADS = [(0, 3), (3, 6), (6, 9), (9, 12), (12, 15), (15, 18)]

        ROPE_ORDER = [0, 8, 1, 2, 9, 3, 4, 10, 5, 6, 11, 7]

        def rope_unit(n):
            return n // ROPED, ROPE_ORDER[n % ROPED]

        def rope_bank(n):
            return 4 + n % 4 if n < ROPED else 4 + n % 2

        def rope_before(n):
            if n < ROPED:
                return n - 4 if n >= 4 else None
            return max(m for m in range(n) if rope_bank(m) == rope_bank(n))

        def rows(i):
            return slice(T0[i], T0[i] + TN[i])

        def half(b):
            return slice(b * HT, (b + 1) * HT)

        def quad(buf, i, c):
            return buf[0:TN[i], i % 2, QUAD * c:QUAD * c + QUAD, 0:TN[i]]

        def quad_bank(n, i):
            return bank[n][0:TN[i], 0:QUAD * TN[i]].rearrange("p (h t) -> p h t", h=QUAD)

        def per_head(buf, i, c):
            return buf[0:TN[i], i, QUAD * c:QUAD * c + QUAD].unsqueeze(2).broadcast_to([TN[i], QUAD, TN[i]])

        UNITS = [(e, b) for b in range(HALVES) for e in range(NSHARED)]
        UNITS += [(e, b) for e in range(NSHARED, NEXP) for b in range(HALVES)]
        NU = len(UNITS)

        def gated_before(u):
            return max(0, u - NSHARED * HALVES)

        def units_until(e):
            return max(u for u, (x, _) in enumerate(UNITS) if x == e) + 1

        def y_bank(b, m):
            return bank[(6, 4)[b] + m]

        block = outer.enter_context(nc.Block())

        @block.sync
        def _(sp):
            def load_projection(c):
                cs = slice(c * CHUNK, (c + 1) * CHUNK)
                sp.dma_start(wqkv_sb[:, :, cs], w_qkv[:, c, :, :]).then_inc(l_qkv[c], 16)

            for b in range(HALVES):
                for k in range(2):
                    ks = slice(k * KP // 2, (k + 1) * KP // 2)
                    if b == 0:
                        sp.dma_start(wp_sb[:, ks, :], wpT[:, ks, :]).then_inc(l_wp[k], 16)
                    sp.dma_start(x_sb[:, b, ks, :], xT[:, b, ks, :]).then_inc(l_x[b][k], 16)
                if b == 0:
                    load_projection(0)
            for c in (2, 1, 3):
                load_projection(c)
            sp.dma_start(wo_sb[:], w_o).then_inc(l_wo, 16)
            for n, (a, z) in enumerate(EXPERT_LOADS):
                if a == EARLY:
                    sp.wait_ge(qk_made, HALVES * ROPED)
                    sp.wait_ge(v_made, TILES)
                dst = ffn_a[:, a:z, :] if a < EARLY else ffn_b[:, a - EARLY:z - EARLY, :]
                sp.dma_start(dst, w_ffn[:, a:z, :]).then_inc(l_ffn[n], 16)
            for i in range(TILES):
                sp.wait_ge(out_made, i + 1)
                sp.dma_start(out[rows(i), :], h[0:TN[i], i, :]).then_inc(s_out, 16)
            sp.wait_ge(s_out, 16 * TILES)

        @block.gpsimd
        def _(pool):
            for n, c in enumerate((0, 2, 1, 3)):
                cs = slice(c * CHUNK, (c + 1) * CHUNK)
                pool.wait_ge(l_qkv[c], 16)
                pool.wait_ge(qkv_hi_made, n + 1)
                nc.gpsimd.tensor_tensor(wqkv_lo[:, :, cs], wqkv_sb[:, :, cs], wqkv_hi[:, :, cs].bitcast(F32),
                                        ALU.subtract).then_inc(qkv_lo_made, 1)

            def sine(n):
                if n == 0:
                    pool.wait_ge(l_rope, 32)
                pool.wait_ge(qk_swapped, n + 1)
                nc.gpsimd.tensor_tensor(swapped[:, n % 3, :], swapped[:, n % 3, :], sin_sb[:],
                                        ALU.mult).then_inc(qk_sin, 1)

            def normalise(i):
                for c in range(2):
                    pool.wait_ge(sc_inv, 2 * i + c + 1)
                    pool.wait_ge(sc_exp, 2 * i + c + 1)
                    nc.gpsimd.tensor_tensor(quad(probs, i, c), quad(probs, i, c), per_head(sinv, i, c),
                                            ALU.mult).then_inc(sc_norm, 1)

            def low_parts(e):
                load = [n for n, (a, z) in enumerate(EXPERT_LOADS) if a <= e < z][0]
                pool.wait_ge(l_ffn[load], 16)
                pool.wait_ge(exp_hi_made, e + 1)
                nc.gpsimd.tensor_tensor(exp_lo[:, e % SPLIT_RING, :], raw_expert(e),
                                        exp_hi[:, e % SPLIT_RING, :].bitcast(F32),
                                        ALU.subtract).then_inc(exp_lo_made, 1)

            for n in range(2 * ROPED):
                sine(n)
                if n == ROPED + 2:
                    normalise(0)
                if n == ROPED + 8:
                    normalise(1)
            for i in range(2, TILES):
                normalise(i)
                if i in (2, 3):
                    low_parts(i - 2)
            for e in range(2, NEXP):
                low_parts(e)

        @block.scalar
        def _(act_e):
            act_e.dma_start(auxw_sb[:], aux_w).then_inc(l_aux, 16)
            act_e.dma_start(auxs_sb[:], aux_sel).then_inc(l_aux, 16)
            act_e.dma_start(ident[:], ident_in).then_inc(l_const, 16)
            act_e.dma_start(mask_f[:], mask_in).then_inc(l_const, 16)
            act_e.dma_start(sel_f[:], sel_in).then_inc(l_const, 16)
            act_e.dma_start(cos_sb[:], cos_t).then_inc(l_rope, 16)
            act_e.dma_start(sin_sb[:], sin_t).then_inc(l_rope, 16)
            act_e.dma_start(wr_sb[:], w_r).then_inc(l_wr, 16)

            def keep_tokens(i):
                act_e.wait_ge(tok_made, i + 1)
                nc.scalar.activation(h[0:TN[i], i, :], bank[i % 2][0:TN[i], 0:HID], ACT.Copy).then_inc(h_kept, 1)

            def inv_std(n):
                r = slice(0, TN[n % TILES])
                act_e.wait_ge(vare_made, n + 1)
                nc.scalar.activation(lnv[r, n:n + 1], vare[r, n:n + 1], ACT.Ln).then_inc(ln_made, 1)
                act_e.wait_ge(ln_made, n + 1)
                nc.scalar.activation(y0[r, n:n + 1], lnv[r, n:n + 1], ACT.Exp, scale=-0.5).then_inc(y0_made, 1)

            def keep_turned(n):
                i = n % TILES
                act_e.wait_ge(hnT_turned, n + 1)
                if n >= TILES:
                    act_e.wait_ge(lo_made, i + 1)
                src = bank[(2 if n < TILES else 4) + i % 2][:, 0:KH * TN[i]].rearrange("p (k t) -> p k t", k=KH)
                nc.scalar.activation(hnT[:, :, rows(i)], src, ACT.Copy).then_inc(hnT_kept, 1)

            def swap(n):
                act_e.wait_ge(qk_made, n + 1)
                if n >= 3:
                    act_e.wait_ge(qk_roped, n - 2)
                ps = bank[rope_bank(n)]
                nc.scalar.activation(swapped[0:64, n % 3, :], ps[64:128, 0:HT], ACT.Copy)
                nc.scalar.activation(swapped[64:128, n % 3, :], ps[0:64, 0:HT], ACT.Copy).then_inc(qk_swapped, 1)

            def keep_v(i):
                act_e.wait_ge(v_made, i + 1)
                nc.scalar.activation(v_sb[0:TN[i], i, :], bank[i % 2][0:TN[i], :], ACT.Copy).then_inc(v_kept, 1)

            def exps(i, c):
                act_e.wait_ge(sc_less, 2 * i + c + 1)
                nc.scalar.activation(quad(probs, i, c), quad(probs, i, c), ACT.Exp, scale=SCALE).then_inc(sc_exp, 1)

            def keep_pT(i):
                for c in range(2):
                    act_e.wait_ge(pT_turned, 2 * i + c + 1)
                    if i >= 2:
                        act_e.wait_ge(pv_made, 2 * (i - 2) + c + 1)
                    nc.scalar.activation(quad(probsT, i, c), quad_bank(6 + c, i), ACT.Copy).then_inc(pT_kept, 1)

            def keep_pv(i):
                for c in range(2):
                    act_e.wait_ge(pv_made, 2 * i + c + 1)
                    src = bank[c][:, 0:QUAD * TN[i]].rearrange("p (h t) -> p h t", h=QUAD)
                    nc.scalar.activation(heads_out[:, QUAD * c:QUAD * c + QUAD, rows(i)], src,
                                         ACT.Copy).then_inc(pv_kept, 1)

            def gelu(u):
                act_e.wait_ge(up_made, u + 1)
                if u >= ACT_RING:
                    act_e.wait_ge(act_lo_made, u - ACT_RING + 1)
                nc.scalar.activation(act[:, u % ACT_RING, :], bank[u % 2][:, 0:HT], ACT.Gelu).then_inc(act_made, 1)

            def act_high(u):
                r = u % ACT_RING
                if u < NSHARED * HALVES:
                    act_e.wait_ge(act_made, u + 1)
                else:
                    act_e.wait_ge(act_gated, gated_before(u) + 1)
                if u >= ACT_RING:
                    act_e.wait_ge(y_made, u - ACT_RING + 1)
                nc.scalar.activation(act_hi[:, r, :], act[:, r, :], ACT.Copy).then_inc(act_hi_made, 1)

            act_e.preload_act_table_set("natural_log_exp_and_others")
            for i in range(TILES):
                keep_tokens(i)
                inv_std(i)
                if i:
                    keep_turned(i - 1)
            for n in range(ROPED):
                swap(n)
                if n == 2:
                    keep_turned(TILES - 1)
            for i in range(3):
                keep_v(i)
            for n in range(6):
                swap(ROPED + n)
                if n < 2:
                    exps(0, n)
            keep_pT(0)
            for n in range(6, ROPED):
                swap(ROPED + n)
                if n < 8:
                    exps(1, n - 6)
            keep_pv(0)
            for i in range(3, TILES):
                keep_v(i)
            for i in range(1, TILES):
                keep_pT(i)
                if i + 1 < TILES:
                    exps(i + 1, 0)
                    exps(i + 1, 1)
                keep_pv(i)
                inv_std(TILES + i - 1)
                if i >= 2:
                    keep_turned(TILES + i - 2)
            inv_std(2 * TILES - 1)
            keep_turned(2 * TILES - 2)
            gelu(0)
            gelu(1)
            keep_turned(2 * TILES - 1)
            act_high(0)
            act_high(1)
            act_e.wait_ge(r_less, 1)
            nc.scalar.activation(rexp[:, :, 0:NROUTED], rlog[:], ACT.Exp).then_inc(r_exp, 1)
            for u in range(2, NU):
                gelu(u)
                if u > 2:
                    act_high(u - 1)
            act_high(NU - 1)
            for m in range(KH):
                act_e.wait_ge(y_made, NU - 1)
                nc.scalar.activation(yT[:, m, half(0)], y_bank(0, m)[:, 0:HT], ACT.Copy).then_inc(yT_kept, 1)
            act_e.wait_ge(y_made, NU)
            for m in range(KH):
                nc.scalar.activation(yT[:, m, half(1)], y_bank(1, m)[:, 0:HT], ACT.Copy).then_inc(yT_kept, 1)

        @block.vector
        def _(dve):
            def qkv_high(n, c):
                cs = slice(c * CHUNK, (c + 1) * CHUNK)
                dve.wait_ge(l_qkv[c], 16)
                nc.vector.tensor_copy(wqkv_hi[:, :, cs], wqkv_sb[:, :, cs]).then_inc(qkv_hi_made, 1)

            def norm_stats(n):
                i = n % TILES
                r = slice(0, TN[i])
                if n < TILES:
                    dve.wait_ge(h_kept, n + 1)
                else:
                    dve.wait_ge(h_added, i + 1)
                nc.vector.bn_stats(stats[r, n, :], h[r, i, :]).then_inc(stats_made, 1)
                dve.wait_ge(stats_made, n + 1)
                nc.vector.bn_aggr(mv[r, n, :], stats[r, n, :]).then_inc(mv_made, 1)
                dve.wait_ge(mv_made, n + 1)
                nc.vector.tensor_scalar(vare[r, n:n + 1], mv[r, n, 1:2], EPS, None, ALU.add).then_inc(vare_made, 1)

            def norm_apply(n):
                i = n % TILES
                r = slice(0, TN[i])
                dve.wait_ge(y0_made, n + 1)
                nc.vector.tensor_tensor(y0y0[r, n:n + 1], y0[r, n:n + 1], y0[r, n:n + 1],
                                        ALU.mult).then_inc(yy_made, 1)
                dve.wait_ge(yy_made, n + 1)
                nc.vector.tensor_scalar(vyy[r, n:n + 1], y0y0[r, n:n + 1], vare[r, n:n + 1], -0.5,
                                        ALU.mult, ALU.mult).then_inc(vyy_made, 1)
                dve.wait_ge(vyy_made, n + 1)
                nc.vector.scalar_tensor_tensor(out=rstd[r, n:n + 1], in0=vyy[r, n:n + 1], scalar=1.5,
                                               in1=y0[r, n:n + 1], op0=ALU.add, op1=ALU.mult).then_inc(rstd_made, 1)
                dve.wait_ge(rstd_made, n + 1)
                if n >= 2:
                    dve.wait_ge(hnT_turned, n - 1)
                nc.vector.tensor_scalar(hn[r, n % 2, :], h[r, i, :], mv[r, n, 0:1], rstd[r, n:n + 1],
                                        ALU.subtract, ALU.mult).then_inc(hn_made, 1)

            def split(n):
                i = n % TILES
                dve.wait_ge(hnT_kept, n + 1)
                if n >= TILES:
                    dve.wait_ge(qk_made, HALVES * ROPED)
                    dve.wait_ge(v_made, TILES)
                nc.vector.tensor_copy(hnT_hi[:, :, rows(i)], hnT[:, :, rows(i)]).then_inc(hi_made, 1)
                dve.wait_ge(hi_made, n + 1)
                nc.vector.tensor_tensor(hnT_lo[:, :, rows(i)], hnT[:, :, rows(i)],
                                        hnT_hi[:, :, rows(i)].bitcast(F32), ALU.subtract).then_inc(lo_made, 1)

            def cosine(n):
                b, head = rope_unit(n)
                if n == 0:
                    dve.wait_ge(l_rope, 32)
                dve.wait_ge(qk_swapped, n + 1)
                nc.vector.tensor_tensor(qk[:, head, half(b)], bank[rope_bank(n)][:, 0:HT], cos_sb[:],
                                        ALU.mult).then_inc(qk_cos, 1)

            def rope_add(n):
                b, head = rope_unit(n)
                dve.wait_ge(qk_cos, n + 1)
                dve.wait_ge(qk_sin, n + 1)
                nc.vector.tensor_tensor(qk[:, head, half(b)], qk[:, head, half(b)], swapped[:, n % 3, :],
                                        ALU.add).then_inc(qk_roped, 1)

            def less_max(i):
                for c in range(2):
                    dve.wait_ge(sc_made, 2 * i + c + 1)
                    nc.vector.tensor_reduce(smax[0:TN[i], i, QUAD * c:QUAD * c + QUAD], quad_bank(2 + c, i),
                                            AX_X, ALU.max).then_inc(sc_max, 1)
                for c in range(2):
                    dve.wait_ge(sc_max, 2 * i + c + 1)
                    if i >= 2:
                        dve.wait_ge(pT_turned, 2 * (i - 2) + c + 1)
                    nc.vector.tensor_tensor(quad(probs, i, c), quad_bank(2 + c, i), per_head(smax, i, c),
                                            ALU.subtract).then_inc(sc_less, 1)

            def inv_sum(i):
                for c in range(2):
                    dve.wait_ge(sc_exp, 2 * i + c + 1)
                    nc.vector.tensor_reduce(ssum[0:TN[i], i, QUAD * c:QUAD * c + QUAD], quad(probs, i, c),
                                            AX_X, ALU.add).then_inc(sc_sum, 1)
                for c in range(2):
                    dve.wait_ge(sc_sum, 2 * i + c + 1)
                    nc.vector.reciprocal(sinv[0:TN[i], i, QUAD * c:QUAD * c + QUAD],
                                         ssum[0:TN[i], i, QUAD * c:QUAD * c + QUAD]).then_inc(sc_inv, 1)

            def add_residual(i):
                dve.wait_ge(wo_made, i + 1)
                r = slice(0, TN[i])
                nc.vector.tensor_tensor(h[r, i, :], bank[4 + i % 2][r, 0:HID], h[r, i, :],
                                        ALU.add).then_inc(h_added, 1)

            def high_parts(e):
                load = [n for n, (a, z) in enumerate(EXPERT_LOADS) if a <= e < z][0]
                dve.wait_ge(l_ffn[load], 16)
                if e == 0:
                    dve.wait_ge(qk_made, HALVES * ROPED)
                    dve.wait_ge(v_made, TILES)
                if e >= SPLIT_RING:
                    dve.wait_ge(y_made, units_until(e - SPLIT_RING))
                nc.vector.tensor_copy(exp_hi[:, e % SPLIT_RING, :], raw_expert(e)).then_inc(exp_hi_made, 1)

            def gates():
                logits = bank[2][0:TMAX, 0:TILES * NROUTED].rearrange("p (i r) -> p i r", i=TILES)
                spread = [TMAX, TILES, NROUTED]
                dve.wait_ge(rl_made, TILES)
                nc.vector.tensor_reduce(rmax[:], logits, AX_X, ALU.max).then_inc(r_max, 1)
                nc.vector.memset(rexp[:, :, NROUTED:], -1.0).then_inc(r_pads, 1)
                dve.wait_ge(r_max, 1)
                nc.vector.tensor_tensor(rlog[:], logits, rmax[:].unsqueeze(2).broadcast_to(spread),
                                        ALU.subtract).then_inc(r_less, 1)
                dve.wait_ge(r_exp, 1)
                dve.wait_ge(r_pads, 1)
                nc.vector.tensor_reduce(rsum[:], rexp[:, :, 0:NROUTED], AX_X, ALU.add).then_inc(r_sum, 1)
                for i in range(TILES):
                    nc.vector.max(rtop[:, i, :], rexp[:, i, :]).then_inc(r_top, 1)
                dve.wait_ge(r_sum, 1)
                nc.vector.reciprocal(rinv[:], rsum[:]).then_inc(r_inv, 1)
                dve.wait_ge(r_top, TILES)
                nc.vector.memset(rtop[:, :, TOPK:], -1.0).then_inc(r_topped, 1)
                dve.wait_ge(r_topped, 1)
                for i in range(TILES):
                    nc.vector.match_replace(rrest[:, i, :], rtop[:, i, :], rexp[:, i, :], 0.0).then_inc(r_rest, 1)
                dve.wait_ge(r_rest, TILES)
                nc.vector.tensor_tensor(rlog[:], rexp[:, :, 0:NROUTED], rrest[:, :, 0:NROUTED],
                                        ALU.subtract).then_inc(r_kept, 1)
                dve.wait_ge(r_kept, 1)
                dve.wait_ge(r_inv, 1)
                nc.vector.tensor_tensor(gate[:, 0], rlog[:], rinv[:].unsqueeze(2).broadcast_to(spread),
                                        ALU.mult).then_inc(r_gate, 1)
                dve.wait_ge(r_gate, 1)
                for s in range(SPLITS):
                    if s:
                        nc.vector.tensor_tensor(gate[:, s], gate[:, s - 1], gparts[:, :, s - 1, :],
                                                ALU.subtract).then_inc(g_part, 1)
                        dve.wait_ge(g_part, 2 * s)
                    nc.vector.tensor_copy(gparts[:, :, s, :], gate[:, s]).then_inc(g_part, 1)
                    dve.wait_ge(g_part, 2 * s + 1)

            def keep_gates():
                dve.wait_ge(g_turned, TILES)
                turned = bank[3][:].bitcast(BF16)
                for i in range(TILES):
                    nc.vector.tensor_copy(gpartsT[:, rows(i)],
                                          turned[0:SPLITS * NROUTED, i * P:i * P + TN[i]]).then_inc(g_kept, 1)

            def gated(u):
                dve.wait_ge(act_made, u + 1)
                dve.wait_ge(gb_made, gated_before(u) + 1)
                nc.vector.tensor_tensor(act[:, u % ACT_RING, :], act[:, u % ACT_RING, :],
                                        bank[2 + u % 2][:, 0:HT], ALU.mult).then_inc(act_gated, 1)

            def act_low(u):
                r = u % ACT_RING
                dve.wait_ge(act_hi_made, u + 1)
                nc.vector.tensor_tensor(act_lo[:, r, :], act[:, r, :], act_hi[:, r, :].bitcast(F32),
                                        ALU.subtract).then_inc(act_lo_made, 1)

            dve.wait_ge(l_const, 48)
            nc.vector.tensor_copy(ident_b[:], ident[:]).then_inc(c_identb, 1)
            nc.vector.tensor_copy(mask_b[:], mask_f[:].unsqueeze(1).broadcast_to([TMAX, QUAD, TMAX])).then_inc(c_mask, 1)
            nc.vector.tensor_copy(sel_b[:], sel_f[:].unsqueeze(2).broadcast_to([SPLITS * NROUTED, NROUTED, P])).then_inc(c_sel, 1)
            for i in range(TILES):
                norm_stats(i)
                if i:
                    split(i - 1)
                norm_apply(i)
                if i < 4:
                    qkv_high(i, (0, 2, 1, 3)[i])
            for n in range(ROPED):
                cosine(n)
                if n:
                    rope_add(n - 1)
                if n == 2:
                    split(TILES - 1)
            rope_add(ROPED - 1)
            less_max(0)
            for n in range(ROPED, 2 * ROPED):
                cosine(n)
                if n > ROPED:
                    rope_add(n - 1)
                if n == ROPED + 1:
                    inv_sum(0)
                if n == ROPED + 5:
                    less_max(1)
                if n == ROPED + 7:
                    inv_sum(1)
            rope_add(2 * ROPED - 1)
            less_max(2)
            for i in range(1, TILES):
                if i + 1 < TILES:
                    inv_sum(i + 1)
                add_residual(i - 1)
                norm_stats(TILES + i - 1)
                if i in (1, 2):
                    high_parts(i - 1)
                if i + 2 < TILES:
                    less_max(i + 2)
                norm_apply(TILES + i - 1)
                if i >= 2:
                    split(TILES + i - 2)
            dve.wait_ge(sc_less, 2 * TILES)
            nc.vector.memset(bank[2][0:TMAX, 0:TILES * NROUTED], 0.0).then_inc(rl_zeroed, 1)
            add_residual(TILES - 1)
            norm_stats(2 * TILES - 1)
            split(2 * TILES - 2)
            norm_apply(2 * TILES - 1)
            high_parts(2)
            split(2 * TILES - 1)
            act_low(0)
            act_low(1)
            gates()
            for u in range(2, NU):
                if u == NSHARED * HALVES:
                    keep_gates()
                if u >= NSHARED * HALVES:
                    gated(u)
                if u > 2:
                    act_low(u - 1)
                if u % HALVES == 0 and u // HALVES + 2 < NEXP:
                    high_parts(u // HALVES + 2)
            act_low(NU - 1)
            for i in range(TILES):
                dve.wait_ge(y_turned, i + 1)
                r = slice(0, TN[i])
                nc.vector.tensor_tensor(h[r, i, :], bank[i % 4][r, 0:HID], h[r, i, :],
                                        ALU.add).then_inc(out_made, 1)

        @block.tensor
        def _(pe):
            def tokens(i):
                b, t = divmod(T0[i], HT)
                ps = bank[i % 2][0:TN[i], 0:HID]
                for k in range(KP):
                    if k % (KP // 2) == 0:
                        if i == 0:
                            pe.wait_ge(l_wp[2 * k // KP], 16)
                        if t == 0:
                            pe.wait_ge(l_x[b][2 * k // KP], 16)
                        if k == 0 and i >= 2:
                            pe.wait_ge(h_kept, i - 1)
                    nc.tensor.matmul(ps, x_sb[:, b, k, t:t + TN[i]], wp_sb[:, k, :], start=(k == 0), stop=False)
                if i == 0:
                    pe.wait_ge(l_aux, 32)
                nc.tensor.matmul(ps, auxs_sb[:, rows(i)], auxw_sb[:], start=False, stop=True).then_inc(tok_made, 1)

            def turn_norm(n):
                i = n % TILES
                if n == 0:
                    pe.wait_ge(l_const, 48)
                pe.wait_ge(hn_made, n + 1)
                if n < TILES:
                    if n >= 2:
                        pe.wait_ge(hnT_kept, n - 1)
                    ps = bank[2 + i % 2]
                else:
                    ps = bank[4 + i % 2]
                for k in range(KH):
                    last = nc.tensor.transpose(ps[:, k * TN[i]:(k + 1) * TN[i]],
                                               hn[0:TN[i], n % 2, k * P:(k + 1) * P], ident[0:TN[i], 0:TN[i]])
                last.then_inc(hnT_turned, 1)

            def three(ps, pairs):
                for n, (a_hi, a_lo, b_hi, b_lo) in enumerate(pairs):
                    for m, (a, b) in enumerate(((a_hi, b_hi), (a_hi, b_lo), (a_lo, b_hi))):
                        last = nc.tensor.matmul(ps, a, b, start=(n == 0 and m == 0),
                                                stop=(n == len(pairs) - 1 and m == 2))
                return last

            def project(n):
                b, head = rope_unit(n)
                if n == 0:
                    pe.wait_ge(lo_made, TILES // 2)
                if n == ROPED:
                    pe.wait_ge(lo_made, TILES)
                if n < ROPED:
                    pe.wait_ge(qkv_lo_made, (1, 3, 2)[head // 4])
                before = rope_before(n)
                if before is not None:
                    pe.wait_ge(qk_cos, before + 1)
                cs = slice(head * D, (head + 1) * D)
                three(bank[rope_bank(n)][:, 0:HT],
                      [(wqkv_hi[:, k, cs], wqkv_lo[:, k, cs], hnT_hi[:, k, half(b)], hnT_lo[:, k, half(b)])
                       for k in range(KH)]).then_inc(qk_made, 1)

            def values(i):
                pe.wait_ge(lo_made, i + 1)
                pe.wait_ge(qkv_lo_made, 4)
                if i >= 2:
                    pe.wait_ge(v_kept, i - 1)
                else:
                    pe.wait_ge(h_kept, TILES)
                if i == 3:
                    pe.wait_ge(pv_kept, 2)
                vs = slice(ROPED * D, QKV)
                three(bank[i % 2][0:TN[i], :],
                      [(hnT_hi[:, k, rows(i)], hnT_lo[:, k, rows(i)], wqkv_hi[:, k, vs], wqkv_lo[:, k, vs])
                       for k in range(KH)]).then_inc(v_made, 1)

            def scores(i):
                b = i // len(GROUPS)
                pe.wait_ge(qk_roped, ROPED * (b + 1))
                if i == 0:
                    pe.wait_ge(c_mask, 1)
                    pe.wait_ge(c_identb, 1)
                    pe.wait_ge(hnT_kept, TILES)
                for c in range(2):
                    if i:
                        pe.wait_ge(sc_less, 2 * (i - 1) + c + 1)
                    nc.tensor.matmul(quad_bank(2 + c, i), ident_b[0:TN[i], 0:TN[i]],
                                     mask_b[0:TN[i], :, 0:TN[i]], start=True, stop=False, skip_group_check=True)
                    for j in range(QUAD):
                        hd = QUAD * c + j
                        last = nc.tensor.matmul(bank[2 + c][0:TN[i], j * TN[i]:(j + 1) * TN[i]],
                                                qk[:, hd, rows(i)], qk[:, NH + hd * NKV // NH, rows(i)],
                                                start=False, stop=(j == QUAD - 1), skip_group_check=True)
                    last.then_inc(sc_made, 1)

            def turn_probs(i):
                for c in range(2):
                    pe.wait_ge(sc_norm, 2 * i + c + 1)
                    if i:
                        pe.wait_ge(pT_kept, 2 * (i - 1) + c + 1)
                    else:
                        pe.wait_ge(qk_cos, ROPED)
                    for j in range(QUAD):
                        last = nc.tensor.transpose(bank[6 + c][0:TN[i], j * TN[i]:(j + 1) * TN[i]],
                                                   probs[0:TN[i], i % 2, QUAD * c + j, 0:TN[i]],
                                                   ident[0:TN[i], 0:TN[i]])
                    last.then_inc(pT_turned, 1)

            def attend(i):
                for c in range(2):
                    pe.wait_ge(pT_kept, 2 * i + c + 1)
                    if i:
                        pe.wait_ge(pv_kept, 2 * (i - 1) + c + 1)
                    if i < 2:
                        pe.wait_ge(v_kept, (3, TILES)[i])
                    for j in range(2):
                        kv = 2 * c + j
                        last = nc.tensor.matmul(
                            bank[c][:, 2 * j * TN[i]:2 * (j + 1) * TN[i]].rearrange("p (h t) -> p h t", h=2),
                            v_sb[0:TN[i], i, kv * D:(kv + 1) * D],
                            probsT[0:TN[i], i % 2, 2 * kv:2 * kv + 2, 0:TN[i]], start=True, stop=True)
                    last.then_inc(pv_made, 1)

            def project_out(i):
                pe.wait_ge(pv_kept, 2 * (i + 1))
                if i == 0:
                    pe.wait_ge(l_wo, 16)
                    pe.wait_ge(qk_cos, HALVES * ROPED)
                if i >= 2:
                    pe.wait_ge(hnT_kept, TILES + i - 1)
                for k in range(NH):
                    last = nc.tensor.matmul(bank[4 + i % 2][0:TN[i], 0:HID], heads_out[:, k, rows(i)], wo_sb[:, k, :],
                                            start=(k == 0), stop=(k == NH - 1))
                last.then_inc(wo_made, 1)

            def route(i):
                if i == 0:
                    pe.wait_ge(l_wr, 16)
                    pe.wait_ge(rl_zeroed, 1)
                pe.wait_ge(hnT_kept, TILES + i + 1)
                for k in range(KH):
                    last = nc.tensor.matmul(bank[2][0:TN[i], i * NROUTED:(i + 1) * NROUTED], hnT[:, k, rows(i)],
                                            wr_sb[:, k, :], start=(k == 0), stop=(k == KH - 1))
                last.then_inc(rl_made, 1)

            def turn_gates():
                pe.wait_ge(g_part, 2 * SPLITS - 1)
                turned = bank[3][:].bitcast(BF16)
                for i in range(TILES):
                    nc.tensor.transpose(turned[0:SPLITS * NROUTED, i * P:i * P + TN[i]],
                                        gparts[0:TN[i], i].rearrange("p s r -> p (s r)"),
                                        ident_b[0:TN[i], 0:TN[i]]).then_inc(g_turned, 1)

            def up(u):
                e, b = UNITS[u]
                s = e % SPLIT_RING
                pe.wait_ge(exp_lo_made, e + 1)
                pe.wait_ge(lo_made, TILES + (b + 1) * TILES // 2)
                if u >= 2:
                    pe.wait_ge(act_made, u - 1)
                else:
                    pe.wait_ge(pv_kept, 2 * TILES)
                three(bank[u % 2][:, 0:HT],
                      [(exp_hi[:, s, k * P:(k + 1) * P], exp_lo[:, s, k * P:(k + 1) * P],
                        hnT_hi[:, k, half(b)], hnT_lo[:, k, half(b)]) for k in range(KH)]).then_inc(up_made, 1)
                if e >= NSHARED:
                    if u == NSHARED * HALVES:
                        pe.wait_ge(g_kept, TILES)
                        pe.wait_ge(c_sel, 1)
                    if gated_before(u) >= 2:
                        pe.wait_ge(act_gated, gated_before(u) - 1)
                    nc.tensor.matmul(bank[2 + u % 2][:, 0:HT], sel_b[:, e - NSHARED, :], gpartsT[:, half(b)],
                                     start=True, stop=True).then_inc(gb_made, 1)

            def down(u):
                e, b = UNITS[u]
                s, r = e % SPLIT_RING, u % ACT_RING
                if e == 0:
                    if b == 0:
                        pe.wait_ge(pT_kept, 2 * TILES)
                    else:
                        pe.wait_ge(hnT_kept, 2 * TILES)
                pe.wait_ge(act_lo_made, u + 1)
                for m in range(KH):
                    ws = slice(KH * P + m * P, KH * P + (m + 1) * P)
                    for n, (w, a) in enumerate(((exp_hi, act_hi), (exp_hi, act_lo), (exp_lo, act_hi))):
                        last = nc.tensor.matmul(y_bank(b, m)[:, 0:HT], w[:, s, ws], a[:, r, :],
                                                start=(e == 0 and n == 0), stop=(e == NEXP - 1 and n == 2))
                last.then_inc(y_made, 1)

            def turn_back(i):
                b = i // len(GROUPS)
                pe.wait_ge(yT_kept, KH * (b + 1))
                if i < 4:
                    pe.wait_ge(act_made, NU)
                    pe.wait_ge(act_gated, NROUTED * HALVES)
                else:
                    pe.wait_ge(out_made, i - 3)
                for m in range(KH):
                    last = nc.tensor.transpose(bank[i % 4][0:TN[i], m * P:(m + 1) * P], yT[:, m, rows(i)], ident[:])
                last.then_inc(y_turned, 1)

            for i in range(TILES):
                tokens(i)
                if i:
                    turn_norm(i - 1)
            for n in range(ROPED):
                project(n)
                if n == 2:
                    turn_norm(TILES - 1)
            for i in range(3):
                values(i)
            scores(0)
            for n in range(6):
                project(ROPED + n)
            scores(1)
            turn_probs(0)
            for n in range(6, ROPED):
                project(ROPED + n)
            attend(0)
            for i in range(3, TILES):
                values(i)
            scores(2)
            for i in range(1, TILES):
                turn_probs(i)
                project_out(i - 1)
                attend(i)
                if i >= 2:
                    turn_norm(TILES + i - 2)
                if i + 2 < TILES:
                    scores(i + 2)
            project_out(TILES - 1)
            turn_norm(2 * TILES - 2)
            up(0)
            up(1)
            turn_norm(2 * TILES - 1)
            LAG = 2
            for u in range(LAG, NU + LAG):
                if u == LAG:
                    for i in range(TILES):
                        route(i)
                if u < NU:
                    if u == NSHARED * HALVES:
                        turn_gates()
                    up(u)
                down(u - LAG)
            for i in range(TILES):
                turn_back(i)


def kernel(x, L0_tok_W, L0_tok_b, L0_tok_cls_token, L0_tok_pos_embedding, L0_attn_Wq, L0_attn_Wk, L0_attn_Wv,
           L0_attn_Wo, L0_ffn_shared_up, L0_ffn_shared_down, L0_ffn_routed_up, L0_ffn_routed_down,
           L0_ffn_router_w):
    import numpy as np
    import concourse.bacc as bacc
    from concourse.bass_utils import run_bass_kernel_spmd

    side = 96 // 16
    px = np.asarray(x).reshape(IMAGES, 3, side, 16, side, 16).transpose(1, 3, 5, 0, 2, 4)
    px = px.reshape(KP, P, IMAGES, PATCHES)
    xT = np.zeros((KP, P, IMAGES, TOKENS), px.dtype)
    xT[:, :, :, 1:] = px
    xT = xT.reshape(KP, P, HALVES, HT).transpose(1, 2, 0, 3)
    wpT = np.asarray(L0_tok_W).reshape(HID, KP, P).transpose(2, 1, 0)

    aux_w = np.concatenate([np.asarray(L0_tok_pos_embedding)[0], np.asarray(L0_tok_b)[None],
                            np.asarray(L0_tok_cls_token)[0]])
    one = np.zeros((TOKENS + 2, TOKENS), np.float32)
    one[:TOKENS] = np.eye(TOKENS)
    one[TOKENS, 1:] = 1
    one[TOKENS + 1, 0] = 1
    aux_sel = np.tile(one, (1, IMAGES))

    w_qkv = np.concatenate([np.asarray(L0_attn_Wq), np.asarray(L0_attn_Wk), np.asarray(L0_attn_Wv)], axis=1)
    w_qkv = w_qkv.reshape(KH, P, QKV // CHUNK, CHUNK).transpose(1, 2, 0, 3)
    w_o = np.asarray(L0_attn_Wo).reshape(NH, P, HID).transpose(1, 0, 2)
    ups = np.concatenate([np.asarray(L0_ffn_shared_up), np.asarray(L0_ffn_routed_up)])
    downs = np.concatenate([np.asarray(L0_ffn_shared_down), np.asarray(L0_ffn_routed_down)])
    ups = ups.reshape(NEXP, P, KH, P).transpose(3, 0, 2, 1).reshape(P, NEXP, KH * P)
    w_ffn = np.concatenate([ups, downs.transpose(2, 0, 1)], axis=2)
    w_r = np.asarray(L0_ffn_router_w).reshape(NROUTED, KH, P).transpose(2, 1, 0)

    inv_freq = (1.0 / 10000.0 ** (np.arange(0, D, 2, dtype=np.float32) / np.float32(D))).astype(np.float32)
    freqs = np.outer(np.arange(TOKENS, dtype=np.float32), inv_freq)
    emb = np.concatenate([freqs, freqs], axis=1).T
    sign = np.where(np.arange(D) < D // 2, -1.0, 1.0)[:, None]
    cos_t = np.tile(np.cos(emb), (1, IMAGES // HALVES))
    sin_t = np.tile(np.sin(emb) * sign, (1, IMAGES // HALVES))
    image, place = np.divmod(np.arange(TMAX), TOKENS)
    allowed = (image[:, None] == image[None]) & (place[None] <= place[:, None])
    mask = np.where(allowed, 0.0, MASKED)
    sel = np.tile(np.eye(NROUTED), (SPLITS, 1))

    arrays = {
        "xT": xT, "wpT": wpT, "aux_w": aux_w, "aux_sel": aux_sel, "w_qkv": w_qkv, "w_o": w_o, "w_ffn": w_ffn,
        "w_r": w_r, "cos_t": cos_t.astype(np.float32), "sin_t": sin_t.astype(np.float32),
        "ident_in": np.eye(P, dtype=np.float32), "mask_in": mask.astype(np.float32), "sel_in": sel.astype(np.float32),
    }
    arrays = {name: np.ascontiguousarray(a) for name, a in arrays.items()}
    nc = bacc.Bacc("TRN2", target_bir_lowering=False, num_devices=1)
    args = [nc.dram_tensor(name, a.shape, mybir.dt.from_np(a.dtype), kind="ExternalInput").ap()
            for name, a in arrays.items()]
    out = nc.dram_tensor("out", (T, HID), F32, kind="ExternalOutput").ap()
    build(nc, *args, out)
    got = run_bass_kernel_spmd(nc, [arrays], core_ids=[0]).results[0]["out"]
    return got.reshape(IMAGES, TOKENS, HID)
```

```python
from contextlib import ExitStack

import concourse.bass as bass
from concourse import mybir

F32 = mybir.dt.float32
F32R = mybir.dt.float32r
BF16 = mybir.dt.bfloat16
ALU = mybir.AluOpType
ACT = mybir.ActivationFunctionType
AX_X = mybir.AxisListType.X

P = 128
IMAGES, PATCHES, TOKENS = 16, 36, 37
HALVES = 2
HT = IMAGES // HALVES * TOKENS
T = IMAGES * TOKENS
GROUPS = (3, 3, 2)
NG = HALVES * len(GROUPS)
GN = [g * TOKENS for g in GROUPS] * HALVES
G0 = [sum(GN[:g]) for g in range(NG)]
GMAX = max(GN)
TILES = -(-T // P)
TN = [min(P, T - i * P) for i in range(TILES)]
HID = 256
KH = HID // P
KP = 3 * 16 * 16 // P
D = 128
NH, NKV = 8, 4
ROPED = NH + NKV
QUAD = 4
NSHARED, NROUTED, TOPK = 2, 16, 4
NEXP = NSHARED + NROUTED
EXPW = KH * P + HID
SPLIT_FROM = 2
SPLIT_RING = 4
WARM_UPS = 7
ACT_RING = 4
PADS = 4
MASKED = -1.0e30
EPS = 1e-5
QKV = (NH + 2 * NKV) * D
CHUNK = 512
SCALE = float(D) ** -0.5


def build(nc, xT, wpT, aux_w, aux_sel, w_qkv, w_o, w_ffn, w_r, cos_t, sin_t, ident_in, mask_in, gate_rows, out):
    outer = ExitStack()
    with outer:
        def sb(name, shape, dt=F32, scope=outer):
            return scope.enter_context(nc.sbuf_tensor(name, shape, dt))

        def sem(name):
            return outer.enter_context(nc.semaphore(name))

        aux_sb = sb("aux_sb", [P, HID])
        aux_parts = sb("aux_parts", [P, HID], F32R)
        aux_high = sb("aux_high", [P, HID], F32R)
        auxs_sb = sb("auxs_sb", [P, TOKENS])
        aux_pick = sb("aux_pick", [P, T], F32R)
        ident = sb("ident", [P, P])
        zeros = sb("zeros", [P, CHUNK], BF16)
        ident_b = sb("ident_b", [P, P], BF16)
        mask_f = sb("mask_f", [GMAX, GMAX])
        mask_b = sb("mask_b", [GMAX, QUAD, GMAX], BF16)
        cos_sb = sb("cos_sb", [P, HT])
        sin_sb = sb("sin_sb", [P, HT])
        wo_hi = sb("wo_hi", [P, NH, HID], F32R)
        wo_lo = sb("wo_lo", [P, NH, HID], F32R)
        wr_sb = sb("wr_sb", [P, KH, NROUTED])
        h = sb("h", [P, TILES, HID])
        hn = sb("hn", [P, 2, HID])
        hnT = sb("hnT", [P, KH, T])
        hnT_hi = sb("hnT_hi", [P, KH, T], F32R)
        hnT_lo = sb("hnT_lo", [P, KH, T], F32R)
        v_sb = sb("v_sb", [P, NG, NKV * D])
        stats = sb("stats", [P, 2 * TILES, 6])
        mv = sb("mv", [P, 2 * TILES, 2])
        vare = sb("vare", [P, 2 * TILES])
        lnv = sb("lnv", [P, 2 * TILES])
        y0 = sb("y0", [P, 2 * TILES])
        y0y0 = sb("y0y0", [P, 2 * TILES])
        vyy = sb("vyy", [P, 2 * TILES])
        rstd = sb("rstd", [P, 2 * TILES])
        smax = sb("smax", [GMAX, NG, NH])
        ssum = sb("ssum", [GMAX, NG, NH])
        sinv = sb("sinv", [GMAX, NG, NH])
        rmax = sb("rmax", [P, TILES])
        rsum = sb("rsum", [P, TILES])
        rinv = sb("rinv", [P, TILES])
        rlog = sb("rlog", [P, TILES, NROUTED])
        rexp = sb("rexp", [P, TILES, NROUTED + PADS])
        rrest = sb("rrest", [P, TILES, NROUTED + PADS])
        rtop = sb("rtop", [P, TILES, 8])
        gate = sb("gate", [P, TILES, NROUTED])
        gateT = sb("gateT", [NROUTED, T])

        early = ExitStack()
        x_sb = sb("x_sb", [P, KP, T], F32, early)
        wp_sb = sb("wp_sb", [P, KP, HID], F32, early)
        early.close()
        spread = ExitStack()
        gates = sb("gates", [P, NROUTED, T], F32, spread)
        spread.close()
        late = ExitStack()
        heads_hi = sb("heads_hi", [P, NH, T], F32R, late)
        heads_lo = sb("heads_lo", [P, NH, T], F32R, late)

        att = ExitStack()
        wqkv_sb = sb("wqkv_sb", [P, KH, QKV], F32, att)
        wqkv_hi = sb("wqkv_hi", [P, KH, QKV], F32R, att)
        wqkv_lo = sb("wqkv_lo", [P, KH, QKV], F32R, att)
        parts = ExitStack()
        wp_hi = sb("wp_hi", [P, KP, HID], F32R, parts)
        wp_lo = sb("wp_lo", [P, KP, HID], F32R, parts)
        x_hi = sb("x_hi", [P, KP, T - SPLIT_FROM * P], F32R, parts)
        x_lo = sb("x_lo", [P, KP, T - SPLIT_FROM * P], F32R, parts)
        parts.close()
        qk = sb("qk", [P, ROPED, T], F32, att)
        swapped = sb("swapped", [P, 3, HT], F32, att)
        unsplit = ExitStack()
        wo_sb = sb("wo_sb", [P, NH, HID], F32, unsplit)
        unsplit.close()
        probs = sb("probs", [GMAX, 2, NH, GMAX], F32, att)
        probsT = sb("probsT", [GMAX, 2, NH, GMAX], F32, att)
        att.close()

        ffn = ExitStack()
        ffn_sb = sb("ffn_sb", [P, NEXP, EXPW], F32, ffn)
        exp_hi = sb("exp_hi", [P, SPLIT_RING, EXPW], F32R, ffn)
        exp_lo = sb("exp_lo", [P, SPLIT_RING, EXPW], F32R, ffn)
        act = sb("act", [P, ACT_RING, HT], F32, ffn)
        act_hi = sb("act_hi", [P, ACT_RING, HT], F32R, ffn)
        act_lo = sb("act_lo", [P, ACT_RING, HT], F32R, ffn)
        yT = sb("yT", [P, KH, T], F32, ffn)
        ffn.close()
        late.close()

        bank = [outer.enter_context(nc.psum_tensor(f"bank{n}", [P, CHUNK], F32)) for n in range(8)]

        l_x = [sem(f"l_x{k}") for k in range(3)]
        l_later_x = [sem(f"l_later_x{n}") for n in range(3)]
        l_wp = [sem(f"l_wp{k}") for k in range(3)]
        l_aux = sem("l_aux")
        l_const = sem("l_const")
        l_qkv = [sem(f"l_qkv{c}") for c in range(QKV // CHUNK)]
        l_rope = sem("l_rope")
        l_wo = sem("l_wo")
        l_wr = sem("l_wr")
        l_ffn = [sem(f"l_ffn{n}") for n in range(6)]
        s_gates = sem("s_gates")
        l_gates = [sem(f"l_gates{n}") for n in range(5)]
        s_out = sem("s_out")
        c_pick = sem("c_pick")
        c_aux_high = sem("c_aux_high")
        c_aux = sem("c_aux")
        c_made = sem("c_made")
        qkv_hi_made = sem("qkv_hi_made")
        qkv_lo_made = sem("qkv_lo_made")
        wo_hi_made = sem("wo_hi_made")
        wo_lo_made = sem("wo_lo_made")
        zeros_made = sem("zeros_made")
        wp_hi_made = sem("wp_hi_made")
        wp_lo_made = sem("wp_lo_made")
        x_hi_made = sem("x_hi_made")
        x_lo_made = sem("x_lo_made")
        tok_made = sem("tok_made")
        h_kept = sem("h_kept")
        stats_made = sem("stats_made")
        mv_made = sem("mv_made")
        vare_made = sem("vare_made")
        ln_made = sem("ln_made")
        y0_made = sem("y0_made")
        yy_made = sem("yy_made")
        vyy_made = sem("vyy_made")
        rstd_made = sem("rstd_made")
        hn_made = sem("hn_made")
        hnT_turned = sem("hnT_turned")
        hnT_kept = sem("hnT_kept")
        hi_made = sem("hi_made")
        lo_made = sem("lo_made")
        qk_made = sem("qk_made")
        qk_swapped = sem("qk_swapped")
        qk_cos = sem("qk_cos")
        qk_sin = sem("qk_sin")
        qk_roped = sem("qk_roped")
        v_made = sem("v_made")
        v_kept = sem("v_kept")
        sc_made = sem("sc_made")
        sc_max = sem("sc_max")
        sc_less = sem("sc_less")
        sc_exp = sem("sc_exp")
        sc_sum = sem("sc_sum")
        sc_inv = sem("sc_inv")
        sc_norm = sem("sc_norm")
        pT_turned = sem("pT_turned")
        pT_kept = sem("pT_kept")
        pv_made = sem("pv_made")
        pv_hi_kept = sem("pv_hi_kept")
        pv_lo_kept = sem("pv_lo_kept")
        wo_made = sem("wo_made")
        h_added = sem("h_added")
        rl_zeroed = sem("rl_zeroed")
        rl_made = sem("rl_made")
        r_max = sem("r_max")
        r_less = sem("r_less")
        r_pads = sem("r_pads")
        r_exp = sem("r_exp")
        r_sum = sem("r_sum")
        r_inv = sem("r_inv")
        r_top = sem("r_top")
        r_topped = sem("r_topped")
        r_rest = sem("r_rest")
        r_kept = sem("r_kept")
        r_gate = sem("r_gate")
        g_turned = sem("g_turned")
        g_kept = sem("g_kept")
        exp_hi_made = sem("exp_hi_made")
        exp_lo_made = sem("exp_lo_made")
        up_made = sem("up_made")
        act_made = sem("act_made")
        act_gated = sem("act_gated")
        act_hi_made = sem("act_hi_made")
        act_lo_made = sem("act_lo_made")
        y_made = sem("y_made")
        y0_kept = sem("y0_kept")
        y1_kept = sem("y1_kept")
        y_turned = sem("y_turned")
        out_made = sem("out_made")

        EXPERT_LOADS = [(a, a + 3) for a in range(0, NEXP, 3)]
        CHUNK_LOADS = [(0, 1), (1, 3), (3, KP)]
        GATE_LOADS = [(0, 1), (1, 2), (2, 4), (4, 10), (10, NROUTED)]
        OUT_STORES = [(0, 2), (2, 4), (4, TILES)]

        QKV_ORDER = (0, 2, 1, 3)

        ROPE_ORDER = [0, 8, 1, 2, 9, 3, 4, 10, 5, 6, 11, 7]

        def split_tile(i):
            return slice((i - SPLIT_FROM) * P, (i - SPLIT_FROM) * P + TN[i])

        def rope_unit(n):
            return n // ROPED, ROPE_ORDER[n % ROPED]

        def rope_bank(n):
            return 4 + n % 4 if n < ROPED else 4 + n % 2

        def rope_before(n):
            if n < ROPED:
                return n - 4 if n >= 4 else None
            return max(m for m in range(n) if rope_bank(m) == rope_bank(n))

        def tile(i):
            return slice(i * P, i * P + TN[i])

        def group(g):
            return slice(G0[g], G0[g] + GN[g])

        def half(b):
            return slice(b * HT, (b + 1) * HT)

        def tiles_with(t):
            return -(-t // P)

        def groups_with(t):
            return sum(G0[g] < t for g in range(NG))

        def quad(buf, g, c):
            return buf[0:GN[g], g % 2, QUAD * c:QUAD * c + QUAD, 0:GN[g]]

        def quad_bank(n, g, rows=None):
            return bank[n][0:rows or GN[g], 0:QUAD * GN[g]].rearrange("p (h t) -> p h t", h=QUAD)

        def per_head(buf, g, c):
            return buf[0:GN[g], g, QUAD * c:QUAD * c + QUAD].unsqueeze(2).broadcast_to([GN[g], QUAD, GN[g]])

        UNITS = [(e, b) for b in range(HALVES) for e in range(NSHARED)]
        UNITS += [(e, b) for e in range(NSHARED, NEXP) for b in range(HALVES)]
        NU = len(UNITS)

        def up_bank(u):
            return u % 2 if u < NSHARED * HALVES else u % 4

        def gated_before(u):
            return max(0, u - NSHARED * HALVES)

        def units_until(e):
            return max(u for u, (x, _) in enumerate(UNITS) if x == e) + 1

        def turned_bank(n):
            return bank[(2 if n < TILES else 4) + n % TILES % 2]

        def y_bank(b, m):
            return bank[(6, 4)[b] + m]

        block = outer.enter_context(nc.Block())

        @block.sync
        def _(sp):
            def load_projection(c):
                cs = slice(c * CHUNK, (c + 1) * CHUNK)
                sp.dma_start(wqkv_sb[:, :, cs], w_qkv[:, c, :, :]).then_inc(l_qkv[c], 16)

            for k, (c, d) in enumerate(CHUNK_LOADS):
                sp.dma_start(wp_sb[:, c:d, :], wpT[:, c:d, :]).then_inc(l_wp[k], 16)
            sp.dma_start(auxs_sb[:], aux_sel).then_inc(l_aux, 16)
            for n, (a, z) in enumerate(((P, 2 * P), (2 * P, 3 * P), (3 * P, T))):
                sp.dma_start(x_sb[:, :, a:z], xT[:, :, a:z]).then_inc(l_later_x[n], 16)
            sp.dma_start(ident[:], ident_in).then_inc(l_const, 16)
            load_projection(QKV_ORDER[0])
            sp.dma_start(mask_f[:], mask_in).then_inc(l_const, 16)
            load_projection(QKV_ORDER[1])
            sp.dma_start(cos_sb[:], cos_t).then_inc(l_rope, 16)
            sp.dma_start(sin_sb[:], sin_t).then_inc(l_rope, 16)
            for c in QKV_ORDER[2:]:
                load_projection(c)
            sp.dma_start(wo_sb[:], w_o).then_inc(l_wo, 16)
            sp.dma_start(wr_sb[:], w_r).then_inc(l_wr, 16)
            sp.wait_ge(qk_made, HALVES * ROPED)
            sp.wait_ge(v_made, NG)
            for n, (a, z) in enumerate(EXPERT_LOADS):
                sp.dma_start(ffn_sb[:, a:z, :], w_ffn[:, a:z, :]).then_inc(l_ffn[n], 16)
            sp.wait_ge(g_kept, 2)
            sp.dma_start(gate_rows, gateT[:]).then_inc(s_gates, 16)
            sp.wait_ge(s_gates, 16)
            for n, (a, z) in enumerate(GATE_LOADS):
                sp.dma_start(gates[:, a:z, :], gate_rows[a:z, :].unsqueeze(0).broadcast_to([P, z - a, T])).then_inc(l_gates[n], 16)
            for a, z in OUT_STORES:
                sp.wait_ge(out_made, z)
                rows = TN[z - 1]
                sp.dma_start(out[a * P:(z - 1) * P + rows, :].rearrange("(i p) c -> p i c", p=rows),
                             h[0:rows, a:z, :]).then_inc(s_out, 16)
            sp.wait_ge(s_out, 16 * len(OUT_STORES))

        @block.gpsimd
        def _(pool):
            def wp_low():
                pool.wait_ge(wp_hi_made, 1)
                nc.gpsimd.tensor_tensor(wp_lo[:], wp_sb[:], wp_hi[:].bitcast(F32), ALU.subtract).then_inc(wp_lo_made, 1)

            def qkv_low(n):
                c = QKV_ORDER[n]
                cs = slice(c * CHUNK, (c + 1) * CHUNK)
                pool.wait_ge(l_qkv[c], 16)
                pool.wait_ge(qkv_hi_made, n + 1)
                nc.gpsimd.tensor_tensor(wqkv_lo[:, :, cs], wqkv_sb[:, :, cs], wqkv_hi[:, :, cs].bitcast(F32),
                                        ALU.subtract).then_inc(qkv_lo_made, 1)

            def wo_low():
                pool.wait_ge(l_wo, 16)
                pool.wait_ge(wo_hi_made, 1)
                nc.gpsimd.tensor_tensor(wo_lo[:], wo_sb[:], wo_hi[:].bitcast(F32), ALU.subtract).then_inc(wo_lo_made, 1)

            def sine(n):
                if n == 0:
                    pool.wait_ge(l_rope, 32)
                pool.wait_ge(qk_swapped, n + 1)
                nc.gpsimd.tensor_tensor(swapped[:, n % 3, :], swapped[:, n % 3, :], sin_sb[:],
                                        ALU.mult).then_inc(qk_sin, 1)

            def normalise(g, c):
                pool.wait_ge(sc_exp, 2 * g + c + 1)
                pool.wait_ge(sc_inv, 2 * g + c + 1)
                nc.gpsimd.tensor_tensor(quad(probs, g, c), quad(probs, g, c), per_head(sinv, g, c),
                                        ALU.mult).then_inc(sc_norm, 1)

            def low_parts(e):
                pool.wait_ge(l_ffn[e // 3], 16)
                pool.wait_ge(exp_hi_made, e + 1)
                if e == 2:
                    pool.wait_ge(sc_made, 2 * NG)
                nc.gpsimd.tensor_tensor(exp_lo[:, e % SPLIT_RING, :], ffn_sb[:, e, :],
                                        exp_hi[:, e % SPLIT_RING, :].bitcast(F32),
                                        ALU.subtract).then_inc(exp_lo_made, 1)

            wp_low()
            for n in range(0, 4):
                qkv_low(n)
            for n in range(0, 8):
                sine(n)
            wo_low()
            for n in range(8, 16):
                sine(n)
            normalise(0, 0)
            sine(16)
            normalise(0, 1)
            normalise(1, 0)
            for n in range(17, 20):
                sine(n)
            normalise(1, 1)
            sine(20)
            normalise(2, 0)
            sine(21)
            normalise(2, 1)
            sine(22)
            sine(23)
            normalise(3, 0)
            normalise(3, 1)
            normalise(4, 0)
            normalise(4, 1)
            normalise(5, 0)
            normalise(5, 1)
            for n in range(0, 8):
                low_parts(n)
            for e in range(8, NEXP):
                low_parts(e)

        @block.scalar
        def _(act_e):
            for k, (c, d) in enumerate(CHUNK_LOADS):
                act_e.dma_start(x_sb[:, c:d, 0:P], xT[:, c:d, 0:P]).then_inc(l_x[k], 16)
            act_e.dma_start(aux_sb[:], aux_w).then_inc(l_aux, 16)

            def qkv_high(n):
                c = QKV_ORDER[n]
                cs = slice(c * CHUNK, (c + 1) * CHUNK)
                act_e.wait_ge(l_qkv[c], 16)
                nc.scalar.activation(wqkv_hi[:, :, cs], wqkv_sb[:, :, cs], ACT.Copy).then_inc(qkv_hi_made, 1)

            def patches_high(i):
                if i < TILES - 1:
                    act_e.wait_ge(l_later_x[i - 1], 16)
                nc.scalar.activation(x_hi[:, :, split_tile(i)], x_sb[:, :, tile(i)], ACT.Copy).then_inc(x_hi_made, 1)

            def keep_tokens(i):
                act_e.wait_ge(tok_made, i + 1)
                nc.scalar.activation(h[0:TN[i], i, :], bank[i % 2][0:TN[i], 0:HID], ACT.Copy).then_inc(h_kept, 1)

            def inv_std(n):
                r = slice(0, TN[n % TILES])
                act_e.wait_ge(vare_made, n + 1)
                nc.scalar.activation(lnv[r, n:n + 1], vare[r, n:n + 1], ACT.Ln).then_inc(ln_made, 1)
                act_e.wait_ge(ln_made, n + 1)
                nc.scalar.activation(y0[r, n:n + 1], lnv[r, n:n + 1], ACT.Exp, scale=-0.5).then_inc(y0_made, 1)

            def keep_turned(n):
                i = n % TILES
                act_e.wait_ge(hnT_turned, n + 1)
                if n >= TILES:
                    act_e.wait_ge(lo_made, i + 1)
                src = turned_bank(n)[:, 0:KH * TN[i]].rearrange("p (k t) -> p k t", k=KH)
                nc.scalar.activation(hnT[:, :, tile(i)], src, ACT.Copy).then_inc(hnT_kept, 1)

            def swap(n):
                act_e.wait_ge(qk_made, n + 1)
                if n >= 3:
                    act_e.wait_ge(qk_roped, n - 2)
                ps = bank[rope_bank(n)]
                nc.scalar.activation(swapped[0:64, n % 3, :], ps[64:128, 0:HT], ACT.Copy)
                nc.scalar.activation(swapped[64:128, n % 3, :], ps[0:64, 0:HT], ACT.Copy).then_inc(qk_swapped, 1)

            def keep_v(g):
                act_e.wait_ge(v_made, g + 1)
                nc.scalar.activation(v_sb[0:GN[g], g, :], bank[g % 2][0:GN[g], :], ACT.Copy).then_inc(v_kept, 1)

            def exps(g, c):
                act_e.wait_ge(sc_less, 2 * g + c + 1)
                nc.scalar.activation(quad(probs, g, c), quad(probs, g, c), ACT.Exp, scale=SCALE).then_inc(sc_exp, 1)

            def keep_pT(g, c):
                act_e.wait_ge(pT_turned, 2 * g + c + 1)
                if g >= 2:
                    act_e.wait_ge(pv_made, 2 * (g - 2) + c + 1)
                nc.scalar.activation(quad(probsT, g, c), quad_bank(6 + c, g), ACT.Copy).then_inc(pT_kept, 1)

            def heads_high(g, c):
                act_e.wait_ge(pv_made, 2 * g + c + 1)
                nc.scalar.activation(heads_hi[:, QUAD * c:QUAD * c + QUAD, group(g)], quad_bank(c, g, P),
                                     ACT.Copy).then_inc(pv_hi_kept, 1)

            def gelu(u):
                act_e.wait_ge(up_made, u + 1)
                if u >= ACT_RING:
                    act_e.wait_ge(act_lo_made, u - ACT_RING + 1)
                nc.scalar.activation(act[:, u % ACT_RING, :], bank[up_bank(u)][:, 0:HT], ACT.Gelu).then_inc(act_made, 1)

            def act_high(u):
                r = u % ACT_RING
                if u < NSHARED * HALVES:
                    act_e.wait_ge(act_made, u + 1)
                else:
                    act_e.wait_ge(act_gated, gated_before(u) + 1)
                if u >= ACT_RING:
                    act_e.wait_ge(y_made, u - ACT_RING + 1)
                nc.scalar.activation(act_hi[:, r, :], act[:, r, :], ACT.Copy).then_inc(act_hi_made, 1)

            def router_exp():
                act_e.wait_ge(r_less, 1)
                nc.scalar.activation(rexp[:, :, 0:NROUTED], rlog[:], ACT.Exp).then_inc(r_exp, 1)

            act_e.preload_act_table_set("natural_log_exp_and_others")
            keep_tokens(0)
            patches_high(2)
            inv_std(0)
            patches_high(3)
            keep_tokens(1)
            patches_high(4)
            qkv_high(0)
            keep_tokens(2)
            inv_std(1)
            qkv_high(1)
            inv_std(2)
            keep_turned(0)
            keep_tokens(3)
            keep_turned(1)
            qkv_high(2)
            keep_turned(2)
            qkv_high(3)
            inv_std(3)
            keep_tokens(4)
            swap(0)
            swap(1)
            inv_std(4)
            keep_turned(3)
            for n in range(2, 8):
                swap(n)
            keep_v(0)
            keep_v(1)
            keep_turned(4)
            keep_v(2)
            for n in range(8, 11):
                swap(n)
            exps(0, 0)
            for n in range(11, 14):
                swap(n)
            keep_v(3)
            swap(14)
            exps(0, 1)
            keep_v(4)
            swap(15)
            swap(16)
            exps(1, 0)
            swap(17)
            keep_v(5)
            swap(18)
            exps(1, 1)
            swap(19)
            exps(2, 0)
            keep_pT(0, 0)
            swap(20)
            keep_pT(0, 1)
            heads_high(0, 0)
            exps(2, 1)
            keep_pT(1, 0)
            swap(21)
            heads_high(0, 1)
            swap(22)
            keep_pT(1, 1)
            heads_high(1, 0)
            swap(23)
            keep_pT(2, 0)
            heads_high(1, 1)
            exps(3, 0)
            exps(3, 1)
            keep_pT(2, 1)
            exps(4, 0)
            heads_high(2, 0)
            keep_pT(3, 0)
            keep_pT(3, 1)
            heads_high(2, 1)
            exps(4, 1)
            heads_high(3, 0)
            inv_std(5)
            keep_pT(4, 0)
            exps(5, 0)
            heads_high(3, 1)
            keep_pT(4, 1)
            keep_turned(5)
            heads_high(4, 0)
            exps(5, 1)
            inv_std(6)
            keep_pT(5, 0)
            heads_high(4, 1)
            keep_pT(5, 1)
            keep_turned(6)
            heads_high(5, 0)
            heads_high(5, 1)
            inv_std(7)
            keep_turned(7)
            inv_std(8)
            keep_turned(8)
            inv_std(9)
            gelu(0)
            keep_turned(9)
            act_high(0)
            gelu(1)
            router_exp()
            act_high(1)
            gelu(2)
            act_high(2)
            gelu(3)
            gelu(4)
            act_high(3)
            gelu(5)
            gelu(6)
            act_high(4)
            gelu(7)
            act_high(5)
            act_high(6)
            gelu(8)
            act_high(7)
            gelu(9)
            gelu(10)
            act_high(8)
            gelu(11)
            act_high(9)
            act_high(10)
            for u in range(12, NU):
                gelu(u)
                act_high(u - 1)
            act_high(NU - 1)
            for b in range(HALVES):
                act_e.wait_ge(y_made, NU - 1 + b)
                nc.scalar.activation(yT[:, 0, half(b)], y_bank(b, 0)[:, 0:HT], ACT.Copy).then_inc(y0_kept, 1)

        @block.vector
        def _(dve):
            def wp_high():
                for n in range(len(CHUNK_LOADS)):
                    dve.wait_ge(l_wp[n], 16)
                nc.vector.tensor_copy(wp_hi[:], wp_sb[:]).then_inc(wp_hi_made, 1)

            def patches_low(i):
                dve.wait_ge(x_hi_made, i - SPLIT_FROM + 1)
                nc.vector.tensor_tensor(x_lo[:, :, split_tile(i)], x_sb[:, :, tile(i)],
                                        x_hi[:, :, split_tile(i)].bitcast(F32), ALU.subtract).then_inc(x_lo_made, 1)

            def norm_stats(n):
                i = n % TILES
                r = slice(0, TN[i])
                if n < TILES:
                    dve.wait_ge(h_kept, n + 1)
                else:
                    dve.wait_ge(h_added, i + 1)
                nc.vector.bn_stats(stats[r, n, :], h[r, i, :]).then_inc(stats_made, 1)
                dve.wait_ge(stats_made, n + 1)
                nc.vector.bn_aggr(mv[r, n, :], stats[r, n, :]).then_inc(mv_made, 1)
                dve.wait_ge(mv_made, n + 1)
                nc.vector.tensor_scalar(vare[r, n:n + 1], mv[r, n, 1:2], EPS, None, ALU.add).then_inc(vare_made, 1)

            def norm_apply(n):
                i = n % TILES
                r = slice(0, TN[i])
                dve.wait_ge(y0_made, n + 1)
                nc.vector.tensor_tensor(y0y0[r, n:n + 1], y0[r, n:n + 1], y0[r, n:n + 1],
                                        ALU.mult).then_inc(yy_made, 1)
                dve.wait_ge(yy_made, n + 1)
                nc.vector.tensor_scalar(vyy[r, n:n + 1], y0y0[r, n:n + 1], vare[r, n:n + 1], -0.5,
                                        ALU.mult, ALU.mult).then_inc(vyy_made, 1)
                dve.wait_ge(vyy_made, n + 1)
                nc.vector.scalar_tensor_tensor(out=rstd[r, n:n + 1], in0=vyy[r, n:n + 1], scalar=1.5,
                                               in1=y0[r, n:n + 1], op0=ALU.add, op1=ALU.mult).then_inc(rstd_made, 1)
                dve.wait_ge(rstd_made, n + 1)
                if n >= 2:
                    dve.wait_ge(hnT_turned, n - 1)
                nc.vector.tensor_scalar(hn[r, n % 2, :], h[r, i, :], mv[r, n, 0:1], rstd[r, n:n + 1],
                                        ALU.subtract, ALU.mult).then_inc(hn_made, 1)

            def split(n):
                i = n % TILES
                dve.wait_ge(hnT_kept, n + 1)
                if n >= TILES:
                    dve.wait_ge(qk_made, HALVES * ROPED)
                    dve.wait_ge(v_made, NG)
                nc.vector.tensor_copy(hnT_hi[:, :, tile(i)], hnT[:, :, tile(i)]).then_inc(hi_made, 1)
                dve.wait_ge(hi_made, n + 1)
                nc.vector.tensor_tensor(hnT_lo[:, :, tile(i)], hnT[:, :, tile(i)],
                                        hnT_hi[:, :, tile(i)].bitcast(F32), ALU.subtract).then_inc(lo_made, 1)

            def cosine(n):
                b, head = rope_unit(n)
                if n == 0:
                    dve.wait_ge(l_rope, 32)
                    dve.wait_ge(tok_made, TILES)
                dve.wait_ge(qk_swapped, n + 1)
                nc.vector.tensor_tensor(qk[:, head, half(b)], bank[rope_bank(n)][:, 0:HT], cos_sb[:],
                                        ALU.mult).then_inc(qk_cos, 1)

            def rope_add(n):
                b, head = rope_unit(n)
                dve.wait_ge(qk_cos, n + 1)
                dve.wait_ge(qk_sin, n + 1)
                nc.vector.tensor_tensor(qk[:, head, half(b)], qk[:, head, half(b)], swapped[:, n % 3, :],
                                        ALU.add).then_inc(qk_roped, 1)

            def rope(first, last):
                for n in range(first, last):
                    cosine(n)
                    if n > first:
                        rope_add(n - 1)
                rope_add(last - 1)

            def less_max(g, c):
                if g == 0 and c == 0:
                    dve.wait_ge(wo_lo_made, 1)
                dve.wait_ge(sc_made, 2 * g + c + 1)
                nc.vector.tensor_reduce(smax[0:GN[g], g, QUAD * c:QUAD * c + QUAD], quad_bank(2 + c, g),
                                        AX_X, ALU.max).then_inc(sc_max, 1)
                dve.wait_ge(sc_max, 2 * g + c + 1)
                if g >= 2:
                    dve.wait_ge(pT_turned, 2 * (g - 2) + c + 1)
                nc.vector.tensor_tensor(quad(probs, g, c), quad_bank(2 + c, g), per_head(smax, g, c),
                                        ALU.subtract).then_inc(sc_less, 1)

            def inv_sum(g, c):
                dve.wait_ge(sc_exp, 2 * g + c + 1)
                nc.vector.tensor_reduce(ssum[0:GN[g], g, QUAD * c:QUAD * c + QUAD], quad(probs, g, c),
                                        AX_X, ALU.add).then_inc(sc_sum, 1)
                dve.wait_ge(sc_sum, 2 * g + c + 1)
                nc.vector.reciprocal(sinv[0:GN[g], g, QUAD * c:QUAD * c + QUAD],
                                     ssum[0:GN[g], g, QUAD * c:QUAD * c + QUAD]).then_inc(sc_inv, 1)

            def heads_low(g, c):
                dve.wait_ge(pv_hi_kept, 2 * g + c + 1)
                hs = slice(QUAD * c, QUAD * c + QUAD)
                nc.vector.tensor_tensor(heads_lo[:, hs, group(g)], quad_bank(c, g, P),
                                        heads_hi[:, hs, group(g)].bitcast(F32), ALU.subtract).then_inc(pv_lo_kept, 1)

            def add_residual(i):
                dve.wait_ge(wo_made, i + 1)
                r = slice(0, TN[i])
                nc.vector.tensor_tensor(h[r, i, :], turned_bank(TILES + i)[r, 0:HID], h[r, i, :],
                                        ALU.add).then_inc(h_added, 1)

            def high_parts(e):
                dve.wait_ge(l_ffn[e // 3], 16)
                if e >= SPLIT_RING:
                    dve.wait_ge(y_made, units_until(e - SPLIT_RING))
                nc.vector.tensor_copy(exp_hi[:, e % SPLIT_RING, :], ffn_sb[:, e, :]).then_inc(exp_hi_made, 1)

            per_expert = [P, TILES, NROUTED]

            def router_less_max():
                logits = bank[2][0:P, 0:TILES * NROUTED].rearrange("p (i r) -> p i r", i=TILES)
                dve.wait_ge(rl_made, TILES)
                nc.vector.tensor_reduce(rmax[:], logits, AX_X, ALU.max).then_inc(r_max, 1)
                nc.vector.memset(rexp[:, :, NROUTED:], -1.0).then_inc(r_pads, 1)
                dve.wait_ge(r_max, 1)
                nc.vector.tensor_tensor(rlog[:], logits, rmax[:].unsqueeze(2).broadcast_to(per_expert),
                                        ALU.subtract).then_inc(r_less, 1)

            def top_gates():
                dve.wait_ge(r_exp, 1)
                dve.wait_ge(r_pads, 1)
                for i in range(TILES):
                    nc.vector.max(rtop[:, i, :], rexp[:, i, :]).then_inc(r_top, 1)
                nc.vector.tensor_reduce(rsum[:], rexp[:, :, 0:NROUTED], AX_X, ALU.add).then_inc(r_sum, 1)
                dve.wait_ge(r_top, TILES)
                nc.vector.memset(rtop[:, :, TOPK:], -1.0).then_inc(r_topped, 1)
                dve.wait_ge(r_sum, 1)
                nc.vector.reciprocal(rinv[:], rsum[:]).then_inc(r_inv, 1)
                dve.wait_ge(r_topped, 1)
                for i in range(TILES):
                    nc.vector.match_replace(rrest[:, i, :], rtop[:, i, :], rexp[:, i, :], 0.0).then_inc(r_rest, 1)
                dve.wait_ge(r_rest, TILES)
                nc.vector.tensor_tensor(rlog[:], rexp[:, :, 0:NROUTED], rrest[:, :, 0:NROUTED],
                                        ALU.subtract).then_inc(r_kept, 1)
                dve.wait_ge(r_kept, 1)
                dve.wait_ge(r_inv, 1)
                nc.vector.tensor_tensor(gate[:], rlog[:], rinv[:].unsqueeze(2).broadcast_to(per_expert),
                                        ALU.mult).then_inc(r_gate, 1)

            def keep_gates():
                for n, (a, z) in enumerate(((0, CHUNK), (CHUNK, T))):
                    dve.wait_ge(g_turned, TILES)
                    nc.vector.tensor_copy(gateT[:, a:z], bank[3 - n][0:NROUTED, 0:z - a]).then_inc(g_kept, 1)

            def gated(u):
                dve.wait_ge(act_made, u + 1)
                e, b = UNITS[u]
                if b == 0 and e - NSHARED in [a for a, _ in GATE_LOADS]:
                    dve.wait_ge(l_gates[[a for a, _ in GATE_LOADS].index(e - NSHARED)], 16)
                nc.vector.tensor_tensor(act[:, u % ACT_RING, :], act[:, u % ACT_RING, :],
                                        gates[:, e - NSHARED, half(b)], ALU.mult).then_inc(act_gated, 1)

            def act_low(u):
                r = u % ACT_RING
                dve.wait_ge(act_hi_made, u + 1)
                nc.vector.tensor_tensor(act_lo[:, r, :], act[:, r, :], act_hi[:, r, :].bitcast(F32),
                                        ALU.subtract).then_inc(act_lo_made, 1)

            def make_zeros():
                nc.vector.memset(zeros[:], 0.0).then_inc(zeros_made, 1)

            def split_added():
                dve.wait_ge(l_aux, 32)
                nc.vector.tensor_copy(aux_high[64:128, :], aux_sb[64:128, :]).then_inc(c_aux_high, 1)
                nc.vector.tensor_copy(aux_pick[:].rearrange("p (i t) -> p i t", t=TOKENS),
                                      auxs_sb[:].unsqueeze(1).broadcast_to([P, IMAGES, TOKENS])).then_inc(c_pick, 1)
                nc.vector.tensor_copy(aux_parts[0:64, :], aux_sb[0:64, :]).then_inc(c_aux, 1)
                dve.wait_ge(c_aux_high, 1)
                nc.vector.tensor_tensor(aux_parts[64:128, :], aux_sb[64:128, :], aux_high[64:128, :].bitcast(F32),
                                        ALU.subtract).then_inc(c_aux, 1)

            def constants(n):
                if n == 0:
                    dve.wait_ge(l_const, 32)
                    nc.vector.tensor_copy(ident_b[:], ident[:]).then_inc(c_made, 1)
                else:
                    nc.vector.tensor_copy(mask_b[:], mask_f[:].unsqueeze(1).broadcast_to([GMAX, QUAD, GMAX])).then_inc(c_made, 1)

            def wo_high():
                dve.wait_ge(l_wo, 16)
                nc.vector.tensor_copy(wo_hi[:], wo_sb[:]).then_inc(wo_hi_made, 1)

            def zero_logits():
                dve.wait_ge(sc_less, 2 * NG)
                nc.vector.memset(bank[2][0:P, 0:TILES * NROUTED], 0.0).then_inc(rl_zeroed, 1)

            make_zeros()
            wp_high()
            split_added()
            norm_stats(0)
            patches_low(2)
            norm_apply(0)
            patches_low(3)
            norm_stats(1)
            patches_low(4)
            norm_stats(2)
            norm_apply(1)
            norm_apply(2)
            for n in range(0, 3):
                split(n)
            norm_stats(3)
            norm_apply(3)
            norm_stats(4)
            cosine(0)
            cosine(1)
            wo_high()
            constants(0)
            rope_add(0)
            cosine(2)
            rope_add(1)
            cosine(3)
            rope_add(2)
            cosine(4)
            rope_add(3)
            rope_add(4)
            cosine(5)
            rope_add(5)
            norm_apply(4)
            cosine(6)
            rope_add(6)
            cosine(7)
            constants(1)
            split(3)
            split(4)
            rope_add(7)
            for n in range(8, 11):
                cosine(n)
            less_max(0, 0)
            rope_add(8)
            rope_add(9)
            inv_sum(0, 0)
            cosine(11)
            rope_add(10)
            rope_add(11)
            cosine(12)
            cosine(13)
            rope_add(12)
            less_max(0, 1)
            rope_add(13)
            cosine(14)
            less_max(1, 0)
            rope_add(14)
            cosine(15)
            inv_sum(0, 1)
            cosine(16)
            rope_add(15)
            inv_sum(1, 0)
            cosine(17)
            rope_add(16)
            less_max(1, 1)
            less_max(2, 0)
            cosine(18)
            rope_add(17)
            inv_sum(1, 1)
            inv_sum(2, 0)
            cosine(19)
            less_max(2, 1)
            rope_add(18)
            cosine(20)
            heads_low(0, 0)
            inv_sum(2, 1)
            rope_add(19)
            cosine(21)
            rope_add(20)
            rope_add(21)
            cosine(22)
            heads_low(0, 1)
            heads_low(1, 0)
            cosine(23)
            rope_add(22)
            rope_add(23)
            less_max(3, 0)
            heads_low(1, 1)
            less_max(3, 1)
            inv_sum(3, 0)
            less_max(4, 0)
            inv_sum(3, 1)
            inv_sum(4, 0)
            less_max(4, 1)
            heads_low(2, 0)
            add_residual(0)
            heads_low(2, 1)
            norm_stats(5)
            less_max(5, 0)
            high_parts(0)
            inv_sum(4, 1)
            inv_sum(5, 0)
            heads_low(3, 0)
            norm_apply(5)
            heads_low(3, 1)
            add_residual(1)
            less_max(5, 1)
            norm_stats(6)
            inv_sum(5, 1)
            zero_logits()
            norm_apply(6)
            heads_low(4, 0)
            heads_low(4, 1)
            add_residual(2)
            high_parts(1)
            norm_stats(7)
            split(5)
            norm_apply(7)
            heads_low(5, 0)
            heads_low(5, 1)
            add_residual(3)
            split(6)
            norm_stats(8)
            split(7)
            norm_apply(8)
            add_residual(4)
            norm_stats(9)
            high_parts(2)
            norm_apply(9)
            split(8)
            split(9)
            router_less_max()
            act_low(0)
            top_gates()
            high_parts(3)
            act_low(1)
            act_low(2)
            keep_gates()
            act_low(3)
            high_parts(4)
            high_parts(5)
            for n in range(4, 7):
                gated(n)
            act_low(4)
            gated(7)
            act_low(5)
            act_low(6)
            gated(8)
            gated(9)
            act_low(7)
            gated(10)
            high_parts(6)
            act_low(8)
            act_low(9)
            gated(11)
            high_parts(7)
            act_low(10)
            for u in range(12, NU):
                gated(u)
                act_low(u - 1)
                if u % HALVES == 1 and u // HALVES + 2 < NEXP:
                    high_parts(u // HALVES + 2)
            act_low(NU - 1)
            for b in range(HALVES):
                dve.wait_ge(y_made, NU - 1 + b)
                nc.vector.tensor_copy(yT[:, 1, half(b)], y_bank(b, 1)[:, 0:HT]).then_inc(y1_kept, 1)
            for i in range(TILES):
                dve.wait_ge(y_turned, i + 1)
                r = slice(0, TN[i])
                nc.vector.tensor_tensor(h[r, i, :], bank[i % 4][r, 0:HID], h[r, i, :],
                                        ALU.add).then_inc(out_made, 1)

        @block.tensor
        def _(pe):
            def three(ps, pairs, more=False):
                for n, (a_hi, a_lo, b_hi, b_lo) in enumerate(pairs):
                    for m, (a, b) in enumerate(((a_hi, b_hi), (a_hi, b_lo), (a_lo, b_hi))):
                        last = nc.tensor.matmul(ps, a, b, start=(n == 0 and m == 0),
                                                stop=(n == len(pairs) - 1 and m == 2 and not more))
                return last

            def warm_up():
                pe.wait_ge(zeros_made, 1)
                for _ in range(WARM_UPS):
                    nc.tensor.matmul(bank[7][:], zeros[:, 0:P], zeros[:], start=True, stop=True)

            def tokens(i):
                ps = bank[i % 2][0:TN[i], 0:HID]
                if i >= SPLIT_FROM:
                    pe.wait_ge(wp_lo_made, 1)
                    pe.wait_ge(x_lo_made, i - SPLIT_FROM + 1)
                    pe.wait_ge(h_kept, i - 1)
                    three(ps, [(x_hi[:, k, split_tile(i)], x_lo[:, k, split_tile(i)], wp_hi[:, k, :], wp_lo[:, k, :])
                               for k in range(KP)], more=True)
                    return
                if i == 1:
                    pe.wait_ge(l_later_x[0], 16)
                for k in range(KP):
                    for n, (first, _) in enumerate(CHUNK_LOADS):
                        if k == first and i == 0:
                            pe.wait_ge(l_wp[n], 16)
                            pe.wait_ge(l_x[n], 16)
                    nc.tensor.matmul(ps, x_sb[:, k, tile(i)], wp_sb[:, k, :], start=(k == 0), stop=False)

            def tokens_added(i):
                if i == 0:
                    pe.wait_ge(c_pick, 1)
                    pe.wait_ge(c_aux, 2)
                nc.tensor.matmul(bank[i % 2][0:TN[i], 0:HID], aux_pick[:, tile(i)], aux_parts[:], start=False,
                                 stop=True).then_inc(tok_made, 1)

            def turn_norm(n):
                i = n % TILES
                if n == 0:
                    pe.wait_ge(l_const, 32)
                pe.wait_ge(hn_made, n + 1)
                if 2 <= n < TILES:
                    pe.wait_ge(hnT_kept, n - 1)
                for k in range(KH):
                    last = nc.tensor.transpose(turned_bank(n)[:, k * TN[i]:(k + 1) * TN[i]],
                                               hn[0:TN[i], n % 2, k * P:(k + 1) * P], ident[0:TN[i], 0:TN[i]])
                last.then_inc(hnT_turned, 1)

            def project(n):
                b, head = rope_unit(n)
                if n % ROPED == 0:
                    pe.wait_ge(lo_made, tiles_with((b + 1) * HT))
                if n < ROPED:
                    pe.wait_ge(qkv_lo_made, QKV_ORDER.index(head * D // CHUNK) + 1)
                before = rope_before(n)
                if before is not None:
                    pe.wait_ge(qk_cos, before + 1)
                cs = slice(head * D, (head + 1) * D)
                three(bank[rope_bank(n)][:, 0:HT],
                      [(wqkv_hi[:, k, cs], wqkv_lo[:, k, cs], hnT_hi[:, k, half(b)], hnT_lo[:, k, half(b)])
                       for k in range(KH)]).then_inc(qk_made, 1)

            def values(g):
                pe.wait_ge(lo_made, tiles_with(G0[g] + GN[g]))
                if g == 0:
                    pe.wait_ge(qkv_lo_made, 4)
                if g >= 2:
                    pe.wait_ge(v_kept, g - 1)
                else:
                    pe.wait_ge(h_kept, TILES)
                vs = slice(ROPED * D, QKV)
                three(bank[g % 2][0:GN[g], :],
                      [(hnT_hi[:, k, group(g)], hnT_lo[:, k, group(g)], wqkv_hi[:, k, vs], wqkv_lo[:, k, vs])
                       for k in range(KH)]).then_inc(v_made, 1)

            def scores(g, c):
                pe.wait_ge(qk_roped, ROPED * (g // len(GROUPS)) + (c + 1) * ROPED // 2)
                if g == 0:
                    pe.wait_ge(c_made, 2)
                    pe.wait_ge(hnT_kept, TILES)
                if g:
                    pe.wait_ge(sc_less, 2 * (g - 1) + c + 1)
                nc.tensor.matmul(quad_bank(2 + c, g), ident_b[0:GN[g], 0:GN[g]],
                                 mask_b[0:GN[g], :, 0:GN[g]], start=True, stop=False, skip_group_check=True)
                for j in range(QUAD):
                    hd = QUAD * c + j
                    last = nc.tensor.matmul(bank[2 + c][0:GN[g], j * GN[g]:(j + 1) * GN[g]],
                                            qk[:, hd, group(g)], qk[:, NH + hd * NKV // NH, group(g)],
                                            start=False, stop=(j == QUAD - 1), skip_group_check=True)
                last.then_inc(sc_made, 1)

            def turn_probs(g, c):
                pe.wait_ge(sc_norm, 2 * g + c + 1)
                if g:
                    pe.wait_ge(pT_kept, 2 * (g - 1) + c + 1)
                else:
                    pe.wait_ge(qk_cos, ROPED)
                for j in range(QUAD):
                    last = nc.tensor.transpose(bank[6 + c][0:GN[g], j * GN[g]:(j + 1) * GN[g]],
                                               probs[0:GN[g], g % 2, QUAD * c + j, 0:GN[g]],
                                               ident[0:GN[g], 0:GN[g]])
                last.then_inc(pT_turned, 1)

            def attend(g, c):
                pe.wait_ge(pT_kept, 2 * g + c + 1)
                if g:
                    pe.wait_ge(pv_lo_kept, 2 * (g - 1) + c + 1)
                else:
                    pe.wait_ge(v_kept, NG)
                for j in range(2):
                    kv = 2 * c + j
                    last = nc.tensor.matmul(
                        bank[c][:, 2 * j * GN[g]:2 * (j + 1) * GN[g]].rearrange("p (h t) -> p h t", h=2),
                        v_sb[0:GN[g], g, kv * D:(kv + 1) * D],
                        probsT[0:GN[g], g % 2, 2 * kv:2 * kv + 2, 0:GN[g]], start=True, stop=True)
                last.then_inc(pv_made, 1)

            def project_out(i):
                pe.wait_ge(pv_lo_kept, 2 * groups_with(i * P + TN[i]))
                if i == 0:
                    pe.wait_ge(wo_lo_made, 1)
                    pe.wait_ge(qk_cos, HALVES * ROPED)
                if i >= 2:
                    pe.wait_ge(hnT_kept, TILES + i - 1)
                three(turned_bank(TILES + i)[0:TN[i], 0:HID],
                      [(heads_hi[:, k, tile(i)], heads_lo[:, k, tile(i)], wo_hi[:, k, :], wo_lo[:, k, :])
                       for k in range(NH)]).then_inc(wo_made, 1)

            def route(i):
                if i == 0:
                    pe.wait_ge(l_wr, 16)
                    pe.wait_ge(rl_zeroed, 1)
                pe.wait_ge(hnT_kept, TILES + i + 1)
                for k in range(KH):
                    last = nc.tensor.matmul(bank[2][0:TN[i], i * NROUTED:(i + 1) * NROUTED], hnT[:, k, tile(i)],
                                            wr_sb[:, k, :], start=(k == 0), stop=(k == KH - 1))
                last.then_inc(rl_made, 1)

            def turn_gates():
                pe.wait_ge(r_gate, 1)
                for i in range(TILES):
                    turned, at = (bank[3], i * P) if i * P < CHUNK else (bank[2], 0)
                    nc.tensor.transpose(turned[0:NROUTED, at:at + TN[i]], gate[0:TN[i], i, :],
                                        ident[0:TN[i], 0:TN[i]]).then_inc(g_turned, 1)

            def up(u):
                e, b = UNITS[u]
                s = e % SPLIT_RING
                pe.wait_ge(exp_lo_made, e + 1)
                pe.wait_ge(lo_made, TILES + tiles_with((b + 1) * HT))
                if u < 2:
                    pe.wait_ge(pv_lo_kept, 2 * NG)
                elif up_bank(u) < 2 or u >= 8:
                    pe.wait_ge(act_made, max(v for v in range(u) if up_bank(v) == up_bank(u)) + 1)
                else:
                    pe.wait_ge(g_kept, 2)
                three(bank[up_bank(u)][:, 0:HT],
                      [(exp_hi[:, s, k * P:(k + 1) * P], exp_lo[:, s, k * P:(k + 1) * P],
                        hnT_hi[:, k, half(b)], hnT_lo[:, k, half(b)]) for k in range(KH)]).then_inc(up_made, 1)

            def down(u):
                e, b = UNITS[u]
                s, r = e % SPLIT_RING, u % ACT_RING
                if e == 0:
                    if b == 0:
                        pe.wait_ge(pT_kept, 2 * NG)
                    else:
                        pe.wait_ge(hnT_kept, 2 * TILES)
                pe.wait_ge(act_lo_made, u + 1)
                for m in range(KH):
                    ws = slice(KH * P + m * P, KH * P + (m + 1) * P)
                    for n, (w, a) in enumerate(((exp_hi, act_hi), (exp_hi, act_lo), (exp_lo, act_hi))):
                        last = nc.tensor.matmul(y_bank(b, m)[:, 0:HT], w[:, s, ws], a[:, r, :],
                                                start=(e == 0 and n == 0), stop=(e == NEXP - 1 and n == 2))
                last.then_inc(y_made, 1)

            def turn_back(i):
                pe.wait_ge(y0_kept, 1 + (i * P + TN[i] > HT))
                pe.wait_ge(y1_kept, 1 + (i * P + TN[i] > HT))
                if i < 4:
                    pe.wait_ge(act_made, NU)
                else:
                    pe.wait_ge(out_made, i - 3)
                for m in range(KH):
                    last = nc.tensor.transpose(bank[i % 4][0:TN[i], m * P:(m + 1) * P], yT[:, m, tile(i)], ident[:])
                last.then_inc(y_turned, 1)

            warm_up()
            tokens(0)
            tokens_added(0)
            tokens(1)
            tokens_added(1)
            tokens(2)
            tokens_added(2)
            tokens(3)
            turn_norm(0)
            tokens_added(3)
            turn_norm(1)
            turn_norm(2)
            tokens(4)
            project(0)
            tokens_added(4)
            for n in range(1, 4):
                project(n)
            turn_norm(3)
            project(4)
            project(5)
            values(0)
            project(6)
            project(7)
            values(1)
            project(8)
            values(2)
            turn_norm(4)
            project(9)
            project(10)
            scores(0, 0)
            values(3)
            for n in range(11, 14):
                project(n)
            values(4)
            scores(0, 1)
            project(14)
            scores(1, 0)
            project(15)
            project(16)
            values(5)
            project(17)
            turn_probs(0, 0)
            scores(1, 1)
            scores(2, 0)
            project(18)
            project(19)
            turn_probs(0, 1)
            scores(2, 1)
            project(20)
            attend(0, 0)
            turn_probs(1, 0)
            project(21)
            turn_probs(1, 1)
            attend(0, 1)
            project(22)
            attend(1, 0)
            project(23)
            turn_probs(2, 0)
            scores(3, 0)
            attend(1, 1)
            attend(2, 0)
            scores(3, 1)
            turn_probs(2, 1)
            scores(4, 0)
            project_out(0)
            scores(4, 1)
            turn_probs(3, 0)
            attend(2, 1)
            turn_probs(3, 1)
            scores(5, 0)
            scores(5, 1)
            attend(3, 0)
            turn_probs(4, 0)
            attend(3, 1)
            project_out(1)
            turn_probs(4, 1)
            attend(4, 0)
            turn_norm(5)
            turn_probs(5, 0)
            attend(4, 1)
            project_out(2)
            turn_probs(5, 1)
            turn_norm(6)
            attend(5, 0)
            attend(5, 1)
            project_out(3)
            turn_norm(7)
            route(0)
            project_out(4)
            up(0)
            turn_norm(8)
            for n in range(1, 4):
                route(n)
            up(1)
            turn_norm(9)
            route(4)
            up(2)
            down(0)
            up(3)
            turn_gates()
            up(4)
            up(5)
            down(1)
            down(2)
            up(6)
            down(3)
            for n in range(7, 12):
                up(n)
            for n in range(4, 9):
                down(n)
            for u in range(12, NU + 3):
                if u < NU:
                    up(u)
                down(u - 3)
            for i in range(TILES):
                turn_back(i)


def kernel(x, L0_tok_W, L0_tok_b, L0_tok_cls_token, L0_tok_pos_embedding, L0_attn_Wq, L0_attn_Wk, L0_attn_Wv,
           L0_attn_Wo, L0_ffn_shared_up, L0_ffn_shared_down, L0_ffn_routed_up, L0_ffn_routed_down,
           L0_ffn_router_w):
    import numpy as np
    import concourse.bacc as bacc
    from concourse.bass_utils import run_bass_kernel_spmd

    side = 96 // 16
    px = np.asarray(x).reshape(IMAGES, 3, side, 16, side, 16).transpose(1, 3, 5, 0, 2, 4)
    px = px.reshape(KP, P, IMAGES, PATCHES)
    xT = np.zeros((KP, P, IMAGES, TOKENS), px.dtype)
    xT[:, :, :, 1:] = px
    xT = xT.reshape(KP, P, T).transpose(1, 0, 2)
    wpT = np.asarray(L0_tok_W).reshape(HID, KP, P).transpose(2, 1, 0)

    added = np.concatenate([np.asarray(L0_tok_pos_embedding)[0], np.asarray(L0_tok_b)[None],
                            np.asarray(L0_tok_cls_token)[0]])
    one = np.zeros((TOKENS + 2, TOKENS), np.float32)
    one[:TOKENS] = np.eye(TOKENS)
    one[TOKENS, 1:] = 1
    one[TOKENS + 1, 0] = 1
    aux_w = np.zeros((2, P // 2, HID), added.dtype)
    aux_w[:, :TOKENS + 2] = added
    aux_w = aux_w.reshape(P, HID)
    aux_sel = np.zeros((2, P // 2, TOKENS), np.float32)
    aux_sel[:, :TOKENS + 2] = one
    aux_sel = aux_sel.reshape(P, TOKENS)

    w_qkv = np.concatenate([np.asarray(L0_attn_Wq), np.asarray(L0_attn_Wk), np.asarray(L0_attn_Wv)], axis=1)
    w_qkv = w_qkv.reshape(KH, P, QKV // CHUNK, CHUNK).transpose(1, 2, 0, 3)
    w_o = np.asarray(L0_attn_Wo).reshape(NH, P, HID).transpose(1, 0, 2)
    ups = np.concatenate([np.asarray(L0_ffn_shared_up), np.asarray(L0_ffn_routed_up)])
    downs = np.concatenate([np.asarray(L0_ffn_shared_down), np.asarray(L0_ffn_routed_down)])
    ups = ups.reshape(NEXP, P, KH, P).transpose(3, 0, 2, 1).reshape(P, NEXP, KH * P)
    w_ffn = np.concatenate([ups, downs.transpose(2, 0, 1)], axis=2)
    w_r = np.asarray(L0_ffn_router_w).reshape(NROUTED, KH, P).transpose(2, 1, 0)

    inv_freq = (1.0 / 10000.0 ** (np.arange(0, D, 2, dtype=np.float32) / np.float32(D))).astype(np.float32)
    freqs = np.outer(np.arange(TOKENS, dtype=np.float32), inv_freq)
    emb = np.concatenate([freqs, freqs], axis=1).T
    sign = np.where(np.arange(D) < D // 2, -1.0, 1.0)[:, None]
    cos_t = np.tile(np.cos(emb), (1, IMAGES // HALVES))
    sin_t = np.tile(np.sin(emb) * sign, (1, IMAGES // HALVES))
    image, place = np.divmod(np.arange(GMAX), TOKENS)
    allowed = (image[:, None] == image[None]) & (place[None] <= place[:, None])
    mask = np.where(allowed, 0.0, MASKED)

    arrays = {
        "xT": xT, "wpT": wpT, "aux_w": aux_w, "aux_sel": aux_sel, "w_qkv": w_qkv, "w_o": w_o, "w_ffn": w_ffn,
        "w_r": w_r, "cos_t": cos_t.astype(np.float32), "sin_t": sin_t.astype(np.float32),
        "ident_in": np.eye(P, dtype=np.float32), "mask_in": mask.astype(np.float32),
    }
    arrays = {name: np.ascontiguousarray(a) for name, a in arrays.items()}
    nc = bacc.Bacc("TRN2", target_bir_lowering=False, num_devices=1)
    args = [nc.dram_tensor(name, a.shape, mybir.dt.from_np(a.dtype), kind="ExternalInput").ap()
            for name, a in arrays.items()]
    gate_rows = nc.dram_tensor("gate_rows", (NROUTED, T), F32, kind="Internal").ap()
    out = nc.dram_tensor("out", (T, HID), F32, kind="ExternalOutput").ap()
    build(nc, *args, gate_rows, out)
    got = run_bass_kernel_spmd(nc, [arrays], core_ids=[0]).results[0]["out"]
    return got.reshape(IMAGES, TOKENS, HID)
```
